# Optimizing a Trainium2 kernel written in Bass

```python
import numpy as np
import jax
import jax.numpy as jnp

def _softmax(x, axis=-1):
    return jax.nn.softmax(x, axis=axis)

def _gelu(x):
    return jax.nn.gelu(x, approximate=True)

def _silu(x):
    return jax.nn.silu(x)

def _sigmoid(x):
    return jax.nn.sigmoid(x)

def _layernorm(x, axis=-1, eps=1e-05):
    m = jnp.mean(x, axis=axis, keepdims=True)
    v = jnp.var(x, axis=axis, keepdims=True)
    return (x - m) / jnp.sqrt(v + eps)

def _scatter_add(tgt, idx, src, axis=0):
    return tgt.at[idx].add(src)

def _segment_sum(src, seg, n):
    return jax.ops.segment_sum(src, seg, n)
kernel_name = 'mk_adaln_attn_ffn_d1_seqx_r8_fc2856'

def setup_inputs(seed: int=0):
    np.random.seed(seed)
    _w = jnp.asarray

    def _rec_inputs():
        import jax
        import jax.numpy as jnp
        _rk = jax.random.key(seed)
        x = -0.000125 + 0.9999 * jax.random.normal(jax.random.fold_in(_rk, 1), (8, 128, 512), jnp.float32)
        _lenS = 128 - jax.random.randint(jax.random.fold_in(_rk, 7), (8,), 0, max(1, 128 // 4) + 1, jnp.int32)
        _lenS2 = 128 - jax.random.randint(jax.random.fold_in(_rk, 8), (8,), 0, max(1, 128 // 4) + 1, jnp.int32)
        itok_B_1_7 = jax.random.randint(jax.random.fold_in(_rk, 11), (8,), 1, 8, jnp.int32)
        itok_Bx16_0_63 = jax.random.randint(jax.random.fold_in(_rk, 12), (8, 16), 0, 64, jnp.int32)
        itok_B_207_1644 = jax.random.randint(jax.random.fold_in(_rk, 13), (8,), 207, 1645, jnp.int32)
        return (x, itok_B_1_7, itok_Bx16_0_63, itok_B_207_1644)
    x, itok_B_1_7, itok_Bx16_0_63, itok_B_207_1644 = _rec_inputs()

    def _L0_cond_setup():
        import jax, jax.numpy as jnp
        import numpy as np
        B, S, D_IN, D_OUT = (4, 256, 512, 512)
        N_ADAPTERS, MAX_RANK = (8, 16)
        key = jax.random.key(seed)
        ks = jax.random.split(key, 7)
        x = jax.random.normal(ks[0], (B, S, D_IN), dtype=jnp.float32)
        weight = jax.random.normal(ks[1], (D_OUT, D_IN), dtype=jnp.float32) * (1.0 / np.sqrt(D_IN))
        bias = jax.random.normal(ks[2], (D_OUT,), dtype=jnp.float32) * 0.01
        lora_a_weights = jax.random.normal(ks[3], (N_ADAPTERS, MAX_RANK, D_IN), dtype=jnp.float32) * (1.0 / np.sqrt(D_IN))
        lora_b_weights = jax.random.normal(ks[4], (N_ADAPTERS, D_OUT, MAX_RANK), dtype=jnp.float32) * 0.02
        scaling_factors = jax.random.uniform(ks[5], (N_ADAPTERS,), dtype=jnp.float32, minval=0.5, maxval=2.0)
        adapter_id = jax.random.randint(ks[6], (B,), 0, N_ADAPTERS, dtype=jnp.int64)
        return {'x': x, 'weight': weight, 'bias': bias, 'lora_a_weights': lora_a_weights, 'lora_b_weights': lora_b_weights, 'scaling_factors': scaling_factors, 'adapter_id': adapter_id}
    _L0_cond_all = _L0_cond_setup()
    _L0_cond_in = {k: v for k, v in _L0_cond_all.items() if k in ('weight', 'bias', 'lora_a_weights', 'lora_b_weights', 'scaling_factors')}
    del _L0_cond_all

    def _L0_attn_setup():
        import jax, jax.numpy as jnp
        import numpy as np
        HIDDEN = 512
        N_HEADS = 32
        N_KV = 8
        HEAD_DIM = HIDDEN // N_HEADS
        Q_PER_KV = N_HEADS // N_KV
        SEQ = 256
        ROPE_BASE = 1000000.0
        POS_SCALE = 1.0
        SM_SCALE = 1.0 / HEAD_DIM
        BLOCK = 64
        LOCAL_BLOCKS = 16
        VERT_STRIDE = 8

        def _blocksparse_mask(seq_len):
            nb = seq_len // BLOCK
            qb = np.arange(nb)[:, None]
            kb = np.arange(nb)[None, :]
            bmask = (kb <= qb) & ((qb - kb < LOCAL_BLOCKS) | ((kb + 1) % VERT_STRIDE == 0))
            emask = np.kron(bmask, np.ones((BLOCK, BLOCK), dtype=bool))
            i = np.arange(seq_len)
            emask &= i[:, None] >= i[None, :]
            return jnp.asarray(emask)

        def _rope(x, cos, sin):
            x1, x2 = jnp.split(x, 2, axis=-1)
            rot = jnp.concatenate([-x2, x1], axis=-1)
            return x * cos[None, :, None, :] + rot * sin[None, :, None, :]
        key = jax.random.key(seed)
        k1, k2, k3, k4, k5 = jax.random.split(key, 5)
        qkv_out = (N_HEADS + 2 * N_KV) * HEAD_DIM
        return {'hidden_states': jax.random.normal(k1, (1, SEQ, HIDDEN), dtype=jnp.float32), 'w_qkv': jax.random.normal(k2, (qkv_out, HIDDEN), dtype=jnp.float32) * 0.02, 'b_qkv': jnp.zeros((qkv_out,), dtype=jnp.float32), 'w_dense': jax.random.normal(k3, (HIDDEN, HIDDEN), dtype=jnp.float32) * 0.02, 'b_dense': jnp.zeros((HIDDEN,), dtype=jnp.float32)}
    _L0_attn_all = _L0_attn_setup()
    _L0_attn_in = {k: v for k, v in _L0_attn_all.items() if k in ('w_qkv', 'b_qkv', 'w_dense', 'b_dense')}
    del _L0_attn_all

    def _L0_cond2_setup():
        import jax, jax.numpy as jnp
        import numpy as np
        B, S, HID = (4, 128, 512)
        D, HQ, HK = (128, 32, 8)
        PAGES, PSIZE, NPP = (64, 32, 16)
        THETA = 10000.0
        EPS = 1e-06
        SCALE = 1.0 / float(np.sqrt(D))

        def _rmsnorm(t, w):
            var = jnp.mean(t * t, axis=-1, keepdims=True)
            return t * jax.lax.rsqrt(var + EPS) * w

        def _rope(t, pos):
            inv_freq = 1.0 / THETA ** (jnp.arange(0, D, 2, dtype=jnp.float32) / D)
            freqs = pos[..., None].astype(jnp.float32) * inv_freq
            cos = jnp.cos(freqs)[:, :, None, :]
            sin = jnp.sin(freqs)[:, :, None, :]
            t1, t2 = (t[..., :D // 2], t[..., D // 2:])
            return jnp.concatenate([t1 * cos - t2 * sin, t2 * cos + t1 * sin], axis=-1)
        key = jax.random.key(seed)
        ks = jax.random.split(key, 10)
        x = jax.random.normal(ks[0], (B, S, HID), jnp.float32)
        Wq = jax.random.normal(ks[1], (HQ * D, HID), jnp.float32) * 0.02
        Wk = jax.random.normal(ks[2], (HK * D, HID), jnp.float32) * 0.02
        Wv = jax.random.normal(ks[3], (HK * D, HID), jnp.float32) * 0.02
        Wo = jax.random.normal(ks[4], (HID, HQ * D), jnp.float32) * 0.02
        q_norm_w = jax.random.uniform(ks[5], (D,), jnp.float32)
        k_norm_w = jax.random.uniform(ks[6], (D,), jnp.float32)
        k_cache = jax.random.normal(ks[7], (PAGES, PSIZE, HK, D), jnp.float32)
        v_cache = jax.random.normal(ks[8], (PAGES, PSIZE, HK, D), jnp.float32)
        block_table = jnp.arange(B * NPP, dtype=jnp.int32).reshape(B, NPP)
        cache_seqlens = jax.random.randint(ks[9], (B,), 0, 475).astype(jnp.int32)
        return dict(x=x, Wq=Wq, Wk=Wk, Wv=Wv, Wo=Wo, q_norm_w=q_norm_w, k_norm_w=k_norm_w, k_cache=k_cache, v_cache=v_cache, block_table=block_table, cache_seqlens=cache_seqlens)
    _L0_cond2_all = _L0_cond2_setup()
    _L0_cond2_in = {k: v for k, v in _L0_cond2_all.items() if k in ('Wq', 'Wk', 'Wv', 'Wo', 'q_norm_w', 'k_norm_w', 'k_cache', 'v_cache')}
    del _L0_cond2_all

    def _L0_ffn_setup():
        import jax, jax.numpy as jnp
        import numpy as np
        RANKS = (8, 16, 32, 64)
        TOPK = 1
        SCALING = 1.0 / 4
        key = jax.random.key(seed)
        ks = jax.random.split(key, 7)
        D_IN, D_OUT, MAX_R, N_RANKS = (512, 512, 64, len(RANKS))
        B_, S_ = (4, 256)
        return {'hidden_states': jax.random.normal(ks[0], (B_, S_, D_IN), jnp.float32), 'W': jax.random.normal(ks[1], (D_OUT, D_IN), jnp.float32) * 0.02, 'b': jax.random.normal(ks[2], (D_OUT,), jnp.float32) * 0.02, 'A': jax.random.normal(ks[3], (MAX_R, D_IN), jnp.float32) * 0.02, 'B': jnp.zeros((D_OUT, MAX_R), jnp.float32) + jax.random.normal(ks[4], (D_OUT, MAX_R), jnp.float32) * 0.02, 'gate_w': jax.random.normal(ks[5], (N_RANKS, D_IN), jnp.float32) * 0.02, 'gate_b': jax.random.normal(ks[6], (N_RANKS,), jnp.float32) * 0.02}
    _L0_ffn_all = _L0_ffn_setup()
    _L0_ffn_in = {k: v for k, v in _L0_ffn_all.items() if k in ('W', 'b', 'A', 'B', 'gate_w', 'gate_b')}
    del _L0_ffn_all
    return {'x': x, 'itok_B_1_7': itok_B_1_7, 'itok_Bx16_0_63': itok_Bx16_0_63, 'itok_B_207_1644': itok_B_207_1644, 'L0_cond_weight': _L0_cond_in['weight'], 'L0_cond_bias': _L0_cond_in['bias'], 'L0_cond_lora_a_weights': _L0_cond_in['lora_a_weights'], 'L0_cond_lora_b_weights': _L0_cond_in['lora_b_weights'], 'L0_cond_scaling_factors': _L0_cond_in['scaling_factors'], 'L0_attn_w_qkv': _L0_attn_in['w_qkv'], 'L0_attn_b_qkv': _L0_attn_in['b_qkv'], 'L0_attn_w_dense': _L0_attn_in['w_dense'], 'L0_attn_b_dense': _L0_attn_in['b_dense'], 'L0_cond2_Wq': _L0_cond2_in['Wq'], 'L0_cond2_Wk': _L0_cond2_in['Wk'], 'L0_cond2_Wv': _L0_cond2_in['Wv'], 'L0_cond2_Wo': _L0_cond2_in['Wo'], 'L0_cond2_q_norm_w': _L0_cond2_in['q_norm_w'], 'L0_cond2_k_norm_w': _L0_cond2_in['k_norm_w'], 'L0_cond2_k_cache': _L0_cond2_in['k_cache'], 'L0_cond2_v_cache': _L0_cond2_in['v_cache'], 'L0_ffn_W': _L0_ffn_in['W'], 'L0_ffn_b': _L0_ffn_in['b'], 'L0_ffn_A': _L0_ffn_in['A'], 'L0_ffn_B': _L0_ffn_in['B'], 'L0_ffn_gate_w': _L0_ffn_in['gate_w'], 'L0_ffn_gate_b': _L0_ffn_in['gate_b']}

def reference(x, itok_B_1_7, itok_Bx16_0_63, itok_B_207_1644, L0_cond_weight, L0_cond_bias, L0_cond_lora_a_weights, L0_cond_lora_b_weights, L0_cond_scaling_factors, L0_attn_w_qkv, L0_attn_b_qkv, L0_attn_w_dense, L0_attn_b_dense, L0_cond2_Wq, L0_cond2_Wk, L0_cond2_Wv, L0_cond2_Wo, L0_cond2_q_norm_w, L0_cond2_k_norm_w, L0_cond2_k_cache, L0_cond2_v_cache, L0_ffn_W, L0_ffn_b, L0_ffn_A, L0_ffn_B, L0_ffn_gate_w, L0_ffn_gate_b):
    import jax
    import jax.numpy as jnp

    def _L0_cond_ref(x, weight, bias, lora_a_weights, lora_b_weights, scaling_factors, adapter_id):
        import jax, jax.numpy as jnp
        import numpy as np
        B, S, D_IN, D_OUT = (4, 256, 512, 512)
        N_ADAPTERS, MAX_RANK = (8, 16)
        base = jnp.einsum('bsi,oi->bso', x, weight) + bias
        a_sel = lora_a_weights[adapter_id]
        b_sel = lora_b_weights[adapter_id]
        scale = scaling_factors[adapter_id]
        low = jnp.einsum('bsi,bri->bsr', x, a_sel)
        delta = jnp.einsum('bsr,bor->bso', low, b_sel)
        return base + scale[:, None, None] * delta

    def _L0_attn_ref(hidden_states, w_qkv, b_qkv, w_dense, b_dense):
        import jax, jax.numpy as jnp
        import numpy as np
        HIDDEN = 512
        N_HEADS = 32
        N_KV = 8
        HEAD_DIM = HIDDEN // N_HEADS
        Q_PER_KV = N_HEADS // N_KV
        SEQ = 256
        ROPE_BASE = 1000000.0
        POS_SCALE = 1.0
        SM_SCALE = 1.0 / HEAD_DIM
        BLOCK = 64
        LOCAL_BLOCKS = 16
        VERT_STRIDE = 8

        def _blocksparse_mask(seq_len):
            nb = seq_len // BLOCK
            qb = np.arange(nb)[:, None]
            kb = np.arange(nb)[None, :]
            bmask = (kb <= qb) & ((qb - kb < LOCAL_BLOCKS) | ((kb + 1) % VERT_STRIDE == 0))
            emask = np.kron(bmask, np.ones((BLOCK, BLOCK), dtype=bool))
            i = np.arange(seq_len)
            emask &= i[:, None] >= i[None, :]
            return jnp.asarray(emask)

        def _rope(x, cos, sin):
            x1, x2 = jnp.split(x, 2, axis=-1)
            rot = jnp.concatenate([-x2, x1], axis=-1)
            return x * cos[None, :, None, :] + rot * sin[None, :, None, :]
        B, S, _ = hidden_states.shape
        qkv = jnp.einsum('bsh,oh->bso', hidden_states, w_qkv) + b_qkv
        qkv = qkv.reshape(B, S, N_KV, Q_PER_KV + 2, HEAD_DIM)
        q = qkv[:, :, :, :Q_PER_KV].reshape(B, S, N_HEADS, HEAD_DIM)
        k = qkv[:, :, :, Q_PER_KV]
        v = qkv[:, :, :, Q_PER_KV + 1]
        inv_freq = 1.0 / ROPE_BASE ** (jnp.arange(0, HEAD_DIM, 2, dtype=jnp.float32) / HEAD_DIM)
        t = jnp.arange(S, dtype=jnp.float32) * POS_SCALE
        freqs = jnp.outer(t, inv_freq)
        emb = jnp.concatenate([freqs, freqs], axis=-1)
        cos, sin = (jnp.cos(emb), jnp.sin(emb))
        q = _rope(q, cos, sin)
        k = _rope(k, cos, sin)
        k = jnp.repeat(k, Q_PER_KV, axis=2)
        v = jnp.repeat(v, Q_PER_KV, axis=2)
        mask = _blocksparse_mask(S)
        scores = jnp.einsum('bqhd,bkhd->bhqk', q, k) * SM_SCALE
        scores = jnp.where(mask[None, None], scores, jnp.finfo(scores.dtype).min)
        probs = jax.nn.softmax(scores, axis=-1)
        ctx = jnp.einsum('bhqk,bkhd->bqhd', probs, v).reshape(B, S, HIDDEN)
        out = jnp.einsum('bsh,oh->bso', ctx, w_dense) + b_dense
        return out

    def _L0_cond2_ref(x, Wq, Wk, Wv, Wo, q_norm_w, k_norm_w, k_cache, v_cache, block_table, cache_seqlens):
        import jax, jax.numpy as jnp
        import numpy as np
        B, S, HID = (4, 128, 512)
        D, HQ, HK = (128, 32, 8)
        PAGES, PSIZE, NPP = (64, 32, 16)
        THETA = 10000.0
        EPS = 1e-06
        SCALE = 1.0 / float(np.sqrt(D))

        def _rmsnorm(t, w):
            var = jnp.mean(t * t, axis=-1, keepdims=True)
            return t * jax.lax.rsqrt(var + EPS) * w

        def _rope(t, pos):
            inv_freq = 1.0 / THETA ** (jnp.arange(0, D, 2, dtype=jnp.float32) / D)
            freqs = pos[..., None].astype(jnp.float32) * inv_freq
            cos = jnp.cos(freqs)[:, :, None, :]
            sin = jnp.sin(freqs)[:, :, None, :]
            t1, t2 = (t[..., :D // 2], t[..., D // 2:])
            return jnp.concatenate([t1 * cos - t2 * sin, t2 * cos + t1 * sin], axis=-1)
        bsz, seqlen, _ = x.shape
        q = jnp.einsum('bsd,ed->bse', x, Wq).reshape(bsz, seqlen, HQ, D)
        k = jnp.einsum('bsd,ed->bse', x, Wk).reshape(bsz, seqlen, HK, D)
        v = jnp.einsum('bsd,ed->bse', x, Wv).reshape(bsz, seqlen, HK, D)
        q = _rmsnorm(q, q_norm_w)
        k = _rmsnorm(k, k_norm_w)
        pos = cache_seqlens[:, None] + jnp.arange(seqlen)[None, :]
        q = _rope(q, pos)
        k = _rope(k, pos)
        L = NPP * PSIZE
        kc = k_cache[block_table].reshape(bsz, L, HK, D)
        vc = v_cache[block_table].reshape(bsz, L, HK, D)
        k_all = jnp.concatenate([kc, k], axis=1)
        v_all = jnp.concatenate([vc, v], axis=1)
        valid_c = jnp.arange(L)[None, :] < cache_seqlens[:, None]
        valid = jnp.concatenate([valid_c, jnp.ones((bsz, seqlen), dtype=bool)], axis=1)
        rep = HQ // HK
        k_all = jnp.repeat(k_all, rep, axis=2)
        v_all = jnp.repeat(v_all, rep, axis=2)
        scores = jnp.einsum('bqhd,bkhd->bhqk', q, k_all) * SCALE
        scores = jnp.where(valid[:, None, None, :], scores, -1e+30)
        probs = jax.nn.softmax(scores, axis=-1)
        o = jnp.einsum('bhqk,bkhd->bqhd', probs, v_all)
        o = o.reshape(bsz, seqlen, HQ * D)
        return jnp.einsum('bse,de->bsd', o, Wo)

    def _L0_ffn_ref(hidden_states, W, b, A, B, gate_w, gate_b):
        import jax, jax.numpy as jnp
        import numpy as np
        RANKS = (8, 16, 32, 64)
        TOPK = 1
        SCALING = 1.0 / 4
        bsz, seq, d_in = hidden_states.shape
        out = jnp.einsum('bsd,od->bso', hidden_states, W) + b
        x = hidden_states.reshape(-1, d_in)
        scores = x @ gate_w.T + gate_b
        probs = jax.nn.softmax(scores, axis=-1)
        routing_weights, selected = jax.lax.top_k(probs, TOPK)
        routing_weights = routing_weights / jnp.sum(routing_weights, axis=-1, keepdims=True)
        lora_outputs = jnp.stack([x @ A[:r, :].T @ B[:, :r].T for r in RANKS], axis=1)
        sel = jnp.take_along_axis(lora_outputs, selected[:, :, None], axis=1)
        final = jnp.sum(sel * routing_weights[:, :, None], axis=1)
        return out + final.reshape(bsz, seq, -1)
    x = x + _L0_attn_ref(_L0_cond_ref(x, L0_cond_weight, L0_cond_bias, L0_cond_lora_a_weights, L0_cond_lora_b_weights, L0_cond_scaling_factors, itok_B_1_7), L0_attn_w_qkv, L0_attn_b_qkv, L0_attn_w_dense, L0_attn_b_dense)
    x = x + _L0_ffn_ref(_L0_cond2_ref(x, L0_cond2_Wq, L0_cond2_Wk, L0_cond2_Wv, L0_cond2_Wo, L0_cond2_q_norm_w, L0_cond2_k_norm_w, L0_cond2_k_cache, L0_cond2_v_cache, itok_Bx16_0_63, itok_B_207_1644), L0_ffn_W, L0_ffn_b, L0_ffn_A, L0_ffn_B, L0_ffn_gate_w, L0_ffn_gate_b)
    return x

_drawn_inputs = setup_inputs


def setup_inputs(seed=0):
    import zlib

    import numpy as np

    out = dict(_drawn_inputs(seed))
    spreads = {'L0_attn_b_qkv': (0.0, 0.1), 'L0_attn_b_dense': (0.0, 0.1)}
    factors = {'L0_cond_bias': 8.0,
     'L0_cond_lora_a_weights': 8.0,
     'L0_cond_lora_b_weights': 8.0,
     'L0_cond_scaling_factors': 8.0,
     'L0_cond2_Wq': 3.651,
     'L0_cond2_Wk': 8.0,
     'L0_cond2_Wv': 8.0,
     'L0_cond2_q_norm_w': 6.299,
     'L0_cond2_k_norm_w': 8.0,
     'L0_cond2_k_cache': 3.668,
     'L0_ffn_b': 183.232,
     'L0_ffn_A': 8.0,
     'L0_ffn_B': 8.0,
     'L0_ffn_gate_w': 8.0,
     'L0_ffn_gate_b': 70.745}
    for name, (base, spread) in spreads.items():
        noise = np.random.default_rng([zlib.crc32(name.encode()), seed]).standard_normal(out[name].shape)
        drawn = base * np.exp(spread * noise) if base else spread * noise
        out[name] = jnp.asarray(drawn.astype(out[name].dtype))
    for name, factor in factors.items():
        out[name] = (out[name] * factor).astype(out[name].dtype)
    return out
```

```python
from contextlib import ExitStack

import numpy as np

import concourse.bass as bass
from concourse import mybir

ALU = mybir.AluOpType
ACT = mybir.ActivationFunctionType
AX = mybir.AxisListType
F32 = mybir.dt.float32
F32R = mybir.dt.float32r
BF16 = mybir.dt.bfloat16
I32 = mybir.dt.int32

P = 128
B, S, D = 8, 128, 512
KT = D // P
H1, G1, D1 = 32, 8, 16
R1 = 16
C1 = 8
QKV1 = (H1 + 2 * G1) * D1
G, REP, HD = 8, 4, 128
PAGES, PSIZE, NPP = 64, 32, 16
L = PSIZE * NPP
LT = L // P
NT = LT + 1
QKV2 = (REP + 2) * HD
SCALE2 = 1.0 / float(np.sqrt(HD))
EPS = 1e-6
MASKED = -1e30
TWO_PI = (6.28125, 0.0019350051879882812, 3.019916050e-07)
RANKS = (8, 16, 32, 64)
MAXR, NR = 64, 4
FF = D + MAXR + NR


def wait(eng, sem, value):
    if isinstance(value, int) and value <= 0:
        return
    eng.wait_ge(sem, value)


def hold(eng):
    eng.nop(nofuse=True)


def wide(ap, n):
    return ap.unsqueeze(2).broadcast_to([ap.shape[0], ap.shape[1], n])


def over(ap, n):
    return ap.unsqueeze(1).broadcast_to([ap.shape[0], n, ap.shape[1]])


def phase1(nc, t, x1t_h, x1t_l, ident, x1_dram, kv_dram):
    with ExitStack() as ctx:
        sb = lambda n, s, d=F32: ctx.enter_context(nc.sbuf_tensor("a_" + n, s, d))
        sem = lambda n: ctx.enter_context(nc.semaphore("a_" + n))
        ps = ctx.enter_context(nc.psum_tensor("a_ps", [P, 8, 512], F32))
        SC, PT, CTX, M0, M1, M2 = (0, 1), (2, 3), 4, 5, 6, 7
        NQK = H1 + G1

        wc = sb("wc", [P, KT, D])
        wq = sb("wq", [P, KT, QKV1])
        wd = sb("wd", [P, KT, D])
        b_cond = sb("b_cond", [P, KT])
        b_qkv = sb("b_qkv", [P, QKV1])
        b_dense = sb("b_dense", [P, D])
        cos = sb("cos", [P, D1])
        sin = sb("sin", [P, D1])
        causal = sb("causal", [P, P])
        blocks = sb("blocks", [P, 8])
        adapters = sb("adapters", [1, B], I32)
        pages = sb("pages", [1, B * NPP], I32)
        la = sb("la", [P, KT, R1])
        lb = sb("lb", [R1, D])
        ls = sb("ls", [R1, 1])
        xt = sb("xt", [P, KT, P])
        xin = sb("xin", [P, D])
        low = sb("low", [R1, P])
        yt = sb("yt", [P, KT, P])
        qkv = sb("qkv", [P, QKV1])
        rope_a = sb("rope_a", [P, NQK, D1])
        rope_b = sb("rope_b", [P, NQK, D1])
        qr = sb("qr", [P, D])
        kr = sb("kr", [P, G1, 4, D1])
        v = sb("v", [P, G1, D1])
        qt = sb("qt", [P, KT, P])
        bd = sb("bd", [P, KT, 8, P])
        sm = sb("sm", [P, 2, 4, P])
        mx = sb("mx", [P, H1])
        nb = sb("nb", [P, H1])
        rs = sb("rs", [P, H1])
        ri = sb("ri", [P, H1])
        pr = sb("pr", [P, 2, 4, P])
        pt = sb("pt", [P, 2, 4, P])
        cx = sb("cx", [P, D])
        cxt = sb("cxt", [P, KT, P])
        xb = sb("xb", [P, D])
        x1 = sb("x1", [P, D])

        weights_in, ids_in = sem("weights_in"), sem("ids_in")
        xt_in, xin_in = sem("xt_in"), sem("xin_in")
        gathered = sem("gathered")
        low_ps, low_sb, yt_ps, yt_sb = sem("low_ps"), sem("low_sb"), sem("yt_ps"), sem("yt_sb")
        q_ps, kv_ps, qkv_sb = sem("q_ps"), sem("kv_ps"), sem("qkv_sb")
        rope_ab, rope_done, v_sb = sem("rope_ab"), sem("rope_done"), sem("v_sb")
        qt_ps, kt_ps, qt_sb, bd_sb = sem("qt_ps"), sem("kt_ps"), sem("qt_sb"), sem("bd_sb")
        sc_ps, masked, bias_sb, exp_done = sem("sc_ps"), sem("masked"), sem("bias_sb"), sem("exp_done")
        pt_ps, pv_done = sem("pt_ps"), sem("pv_done")
        pt_sb = [sem("pt_sb_dve"), sem("pt_sb_act")]
        ri_sb, cx_sb, cxt_ps, cxt_sb = sem("ri_sb"), sem("cx_sb"), sem("cxt_ps"), sem("cxt_sb")
        de_ps, xb_sb, x1_sb, x1_out = sem("de_ps"), sem("xb_sb"), sem("x1_sb"), sem("x1_out")
        xt_ps, xh_sb, xl_sb = sem("xt_ps"), sem("xh_sb"), sem("xl_sb")

        def slots(eng, slot):
            slot(0)
            with eng.Fori(1, B - 1) as b:
                slot(b)
            slot(B - 1)

        def has_next(b):
            return not (isinstance(b, int) and b == B - 1)

        def has_last(b):
            return not (isinstance(b, int) and b == 0)

        block = ctx.enter_context(nc.Block())
        weights = ((wc, "wc"), (b_cond, "b_cond"), (wq, "wq"), (b_qkv, "b_qkv"), (cos, "cos"), (sin, "sin"),
                   (ident, "ident"), (blocks, "blocks"), (causal, "causal"), (wd, "wd"), (b_dense, "b_dense"))

        @block.sync
        def _(sp):
            sp.dma_start(adapters[:], t["adapters"]).then_inc(ids_in, 16)
            sp.dma_start(pages[:], t["pages"]).then_inc(ids_in, 16)

            def load(b):
                wait(sp, yt_ps, b)
                wait(sp, low_sb, b)
                sp.dma_start(xt[:], t["xt"][:, :, bass.ds(b, 1), :].rearrange("p k b s -> p k (b s)")).then_inc(xt_in, 16)
                a = sp.value_load(adapters[0:1, bass.ds(b, 1)], min_val=0, max_val=7)
                sp.dma_start(la[:], t["la"][bass.ds(a, 1)].rearrange("a (k p) r -> p (a k) r", p=P)).then_inc(xt_in, 16)
                sp.dma_start(lb[:], t["lb"][bass.ds(a, 1)].rearrange("a r o -> (a r) o")).then_inc(xt_in, 16)
                sp.dma_start(ls[:], t["ls"][bass.ds(a, 1)].rearrange("a r o -> (a r) o")).then_inc(xt_in, 16)

            def load_in(b):
                wait(sp, xb_sb, b)
                sp.dma_start(xin[:], t["x"][bass.ds(b, 1)].rearrange("b s d -> (b s) d")).then_inc(xin_in, 16)

            def store(b):
                sp.wait_ge(x1_sb, b + 1)
                sp.dma_start(x1_dram[bass.ds(b, 1)].rearrange("b s d -> (b s) d"), x1[:]).then_inc(x1_out, 16)

            def gather(b):
                for j in range(NPP):
                    page = sp.value_load(pages[0:1, bass.ds(b * NPP + j, 1)], min_val=0, max_val=PAGES - 1)
                    sp.dma_start(kv_dram[bass.ds(b, 1), :, j * PSIZE:(j + 1) * PSIZE].rearrange("b g s d -> (b g) (s d)"),
                                 t["kv"][bass.ds(page, 1)].rearrange("a g s d -> (a g) (s d)")).then_inc(gathered, 16)

            sp.wait_ge(ids_in, 32)
            load(0)
            for dst, name in weights:
                sp.dma_start(dst[:], t[name]).then_inc(weights_in, 16)

            def slot(b):
                if has_next(b):
                    load(b + 1)
                if has_last(b):
                    store(b - 1)
                load_in(b)
                gather(b)

            slots(sp, slot)
            store(B - 1)
            sp.wait_ge(gathered, 16 * B * NPP)
            sp.wait_ge(x1_out, 16 * B)

        @block.tensor
        def _(pe):
            def low_rank(a):
                pe.wait_ge(xt_in, 64 * (a + 1))
                wait(pe, xl_sb, a - 2)
                for k in range(KT):
                    mm = pe.matmul(ps[0:R1, M0, 0:P], la[:, k], xt[:, k], start=k == 0, stop=k == KT - 1)
                mm.then_inc(low_ps, 1)

            def cond(a):
                pe.wait_ge(low_sb, a + 1)
                wait(pe, qt_sb, a)
                for o in range(KT):
                    for k in range(KT):
                        pe.matmul(ps[:, M1, o * P:(o + 1) * P], wc[:, k, o * P:(o + 1) * P], xt[:, k],
                                  start=k == 0, stop=False)
                    mm = pe.matmul(ps[:, M1, o * P:(o + 1) * P], lb[:, o * P:(o + 1) * P], low[:], start=False, stop=True)
                mm.then_inc(yt_ps, 1)

            def project(a):
                pe.wait_ge(yt_sb, a + 1)
                wait(pe, cxt_sb, a - 1)
                for k in range(KT):
                    mm = pe.matmul(ps[:, M2, :], yt[:, k], wq[:, k, 0:D], start=k == 0, stop=k == KT - 1)
                mm.then_inc(q_ps, 1)
                for k in range(KT):
                    mm = pe.matmul(ps[:, M1, 0:QKV1 - D], yt[:, k], wq[:, k, D:], start=k == 0, stop=k == KT - 1)
                mm.then_inc(kv_ps, 1)

            def turn(a):
                pe.wait_ge(rope_done, a + 1)
                for k in range(KT):
                    mm = pe.transpose(ps[:, M1, k * P:(k + 1) * P], qr[:, k * P:(k + 1) * P], ident[:])
                mm.then_inc(qt_ps, 1)
                flat = kr[:].rearrange("p g j d -> p (g j d)")
                for k in range(KT):
                    mm = pe.transpose(ps[:, M2, k * P:(k + 1) * P], flat[:, k * P:(k + 1) * P], ident[:])
                mm.then_inc(kt_ps, 1)

            def scores(b, c):
                if c == 0:
                    pe.wait_ge(qt_sb, b + 1)
                    pe.wait_ge(bd_sb, b + 1)
                wait(pe, masked, 8 * b + c - 1)
                pe.matmul(ps[:, SC[c % 2], :], qt[:, c // 2], bd[:, c // 2, 4 * (c % 2):4 * (c % 2) + 4].rearrange("p j s -> p (j s)"),
                          start=True, stop=True).then_inc(sc_ps, 1)

            def turn_probs(b, c):
                pe.wait_ge(exp_done, 8 * b + c + 1)
                n = 4 * b + c // 2
                wait(pe, pt_sb[c % 2], n)
                for j in range(4):
                    mm = pe.transpose(ps[:, PT[c % 2], j * P:(j + 1) * P], pr[:, c % 2, j], ident[:])
                mm.then_inc(pt_ps, 1)

            def context(b, c):
                if c == 0:
                    wait(pe, cx_sb, b)
                    pe.wait_ge(v_sb, b + 1)
                pe.wait_ge(pt_sb[c % 2], 4 * b + c // 2 + 1)
                for j in range(4):
                    h = 4 * c + j
                    mm = pe.matmul(ps[:, CTX, h * D1:(h + 1) * D1], pt[:, c % 2, j], v[:, c], start=True, stop=True)
                mm.then_inc(pv_done, 1)

            def turn_context(d):
                pe.wait_ge(cx_sb, d + 1)
                wait(pe, bd_sb, d + 2 if has_next(d) else d + 1)
                for k in range(KT):
                    mm = pe.transpose(ps[:, M2, k * P:(k + 1) * P], cx[:, k * P:(k + 1) * P], ident[:])
                mm.then_inc(cxt_ps, 1)

            def dense(d):
                pe.wait_ge(cxt_sb, d + 1)
                if has_next(d + 1) and has_next(d):
                    pe.wait_ge(low_sb, d + 3)
                wait(pe, xl_sb, d)
                for k in range(KT):
                    mm = pe.matmul(ps[:, M0, :], cxt[:, k], wd[:, k], start=k == 0, stop=k == KT - 1)
                mm.then_inc(de_ps, 1)

            def turn_x1(d):
                pe.wait_ge(x1_sb, d + 1)
                for k in range(KT):
                    mm = pe.transpose(ps[:, M0, k * P:(k + 1) * P], x1[:, k * P:(k + 1) * P], ident[:])
                mm.then_inc(xt_ps, 1)

            def slot(b):
                nxt, last = has_next(b), has_last(b)
                scores(b, 0)
                if nxt:
                    low_rank(b + 1)
                scores(b, 1)
                if last:
                    turn_context(b - 1)
                if nxt:
                    cond(b + 1)
                turn_probs(b, 0)
                scores(b, 2)
                turn_probs(b, 1)
                if last:
                    dense(b - 1)
                scores(b, 3)
                context(b, 0)
                turn_probs(b, 2)
                if nxt:
                    project(b + 1)
                scores(b, 4)
                context(b, 1)
                turn_probs(b, 3)
                scores(b, 5)
                context(b, 2)
                turn_probs(b, 4)
                if last:
                    turn_x1(b - 1)
                scores(b, 6)
                context(b, 3)
                turn_probs(b, 5)
                scores(b, 7)
                context(b, 4)
                turn_probs(b, 6)
                if nxt:
                    turn(b + 1)
                context(b, 5)
                turn_probs(b, 7)
                context(b, 6)
                context(b, 7)

            pe.wait_ge(weights_in, 16 * len(weights))
            low_rank(0)
            cond(0)
            project(0)
            turn(0)
            slots(pe, slot)
            turn_context(B - 1)
            dense(B - 1)
            turn_x1(B - 1)

        @block.scalar
        def _(act):
            def low_out(a):
                act.wait_ge(low_ps, a + 1)
                wait(act, yt_ps, a)
                act.activation(low[:], ps[0:R1, M0, 0:P], ACT.Copy, scale=ls[:, 0:1]).then_inc(low_sb, 1)

            def y_out(a):
                act.wait_ge(yt_ps, a + 1)
                wait(act, kv_ps, a)
                for o in range(KT):
                    op = act.activation(yt[:, o], ps[:, M1, o * P:(o + 1) * P], ACT.Identity, bias=b_cond[:, o:o + 1])
                op.then_inc(yt_sb, 1)

            def qt_out(a):
                act.wait_ge(qt_ps, a + 1)
                wait(act, sc_ps, 8 * a)
                act.activation(qt[:].rearrange("p k s -> p (k s)"), ps[:, M1, :], ACT.Copy).then_inc(qt_sb, 1)

            def exponent(b, c):
                act.wait_ge(bias_sb, 8 * b + c + 1)
                wait(act, pt_ps, 8 * b + c - 1)
                for j in range(4):
                    h = 4 * c + j
                    op = act.activation(pr[:, c % 2, j], sm[:, c % 2, j], ACT.Exp, bias=nb[:, h:h + 1],
                                        scale=1.0 / D1, accum_out=rs[:, h:h + 1])
                op.then_inc(exp_done, 1)

            def probs_out(b, c):
                act.wait_ge(pt_ps, 8 * b + c + 1)
                wait(act, pv_done, 8 * b + c - 1)
                act.activation(pt[:, c % 2].rearrange("p j s -> p (j s)"), ps[:, PT[c % 2], :], ACT.Copy).then_inc(pt_sb[1], 1)

            def context_out(d):
                act.wait_ge(cxt_ps, d + 1)
                wait(act, de_ps, d)
                act.activation(cxt[:].rearrange("p k s -> p (k s)"), ps[:, M2, :], ACT.Copy).then_inc(cxt_sb, 1)

            def x1_high(d):
                act.wait_ge(xt_ps, d + 1)
                act.activation(x1t_h[:, bass.ds(d, 1)].rearrange("p b k s -> p (b k s)"), ps[:, M0, :], ACT.Copy).then_inc(xh_sb, 1)

            def slot(b):
                nxt, last = has_next(b), has_last(b)
                if nxt:
                    low_out(b + 1)
                exponent(b, 0)
                if last:
                    context_out(b - 1)
                if nxt:
                    y_out(b + 1)
                exponent(b, 1)
                exponent(b, 2)
                probs_out(b, 1)
                exponent(b, 3)
                exponent(b, 4)
                probs_out(b, 3)
                exponent(b, 5)
                if last:
                    x1_high(b - 1)
                exponent(b, 6)
                probs_out(b, 5)
                exponent(b, 7)
                if nxt:
                    qt_out(b + 1)
                probs_out(b, 7)

            act.wait_ge(weights_in, 16 * len(weights))
            low_out(0)
            y_out(0)
            qt_out(0)
            slots(act, slot)
            context_out(B - 1)
            x1_high(B - 1)

        @block.vector
        def _(dve):
            def qkv_out(a):
                dve.wait_ge(q_ps, a + 1)
                wait(dve, rope_ab, a)
                wait(dve, v_sb, a)
                dve.tensor_tensor(qkv[:, 0:D], ps[:, M2, :], b_qkv[:, 0:D], ALU.add)
                dve.wait_ge(kv_ps, a + 1)
                dve.tensor_tensor(qkv[:, D:], ps[:, M1, 0:QKV1 - D], b_qkv[:, D:], ALU.add).then_inc(qkv_sb, 1)

            def rope_sum(a):
                dve.wait_ge(rope_ab, a + 1)
                wait(dve, kt_ps, a)
                dve.tensor_tensor(qr[:], rope_a[:, 0:H1].rearrange("p h d -> p (h d)"),
                                  rope_b[:, 0:H1].rearrange("p h d -> p (h d)"), ALU.add)
                shape = [P, G1, 4, D1]
                dve.tensor_tensor(kr[:], rope_a[:, H1:].unsqueeze(2).broadcast_to(shape),
                                  rope_b[:, H1:].unsqueeze(2).broadcast_to(shape), ALU.add).then_inc(rope_done, 1)

            def keys_out(a):
                dve.wait_ge(kt_ps, a + 1)
                wait(dve, sc_ps, 8 * a)
                for k in range(KT):
                    op = dve.tensor_tensor(bd[:, k], over(ps[:, M2, k * P:(k + 1) * P], 8), wide(blocks[:], P), ALU.mult)
                op.then_inc(bd_sb, 1)

            def mask(b, c):
                dve.wait_ge(sc_ps, 8 * b + c + 1)
                wait(dve, exp_done, 8 * b + c - 1)
                hold(dve)
                for j in range(4):
                    h = 4 * c + j
                    op = dve.tensor_tensor_reduce(sm[:, c % 2, j], ps[:, SC[c % 2], j * P:(j + 1) * P], causal[:], 1.0, MASKED,
                                                  ALU.add, ALU.max, mx[:, h:h + 1])
                op.then_inc(masked, 1)
                dve.wait_ge(masked, 8 * b + c + 1)
                dve.tensor_scalar(nb[:, 4 * c:4 * c + 4], mx[:, 4 * c:4 * c + 4], -1.0 / D1, None, ALU.mult).then_inc(bias_sb, 1)

            def probs_out(b, c):
                dve.wait_ge(pt_ps, 8 * b + c + 1)
                wait(dve, pv_done, 8 * b + c - 1)
                dve.tensor_copy(pt[:, c % 2].rearrange("p j s -> p (j s)"), ps[:, PT[c % 2], :]).then_inc(pt_sb[0], 1)

            def normalize(b):
                dve.wait_ge(exp_done, 8 * (b + 1))
                dve.reciprocal(ri[:], rs[:]).then_inc(ri_sb, 1)
                dve.wait_ge(ri_sb, b + 1)
                dve.wait_ge(pv_done, 8 * (b + 1))
                wait(dve, cxt_ps, b)
                dve.tensor_tensor(cx[:].rearrange("p (h d) -> p h d", d=D1), ps[:, CTX, :].rearrange("p (h d) -> p h d", d=D1),
                                  wide(ri[:], D1), ALU.mult).then_inc(cx_sb, 1)

            def residual(d):
                dve.wait_ge(de_ps, d + 1)
                dve.wait_ge(xb_sb, d + 1)
                wait(dve, xt_ps, d)
                wait(dve, x1_out, 16 * d)
                dve.tensor_tensor(x1[:], ps[:, M0, :], xb[:], ALU.add).then_inc(x1_sb, 1)

            def x1_rest(d):
                dve.wait_ge(xh_sb, d + 1)
                dve.tensor_tensor(x1t_l[:, bass.ds(d, 1)].rearrange("p b k s -> p (b k s)"), ps[:, M0, :],
                                  x1t_h[:, bass.ds(d, 1)].rearrange("p b k s -> p (b k s)"), ALU.subtract).then_inc(xl_sb, 1)

            def slot(b):
                nxt, last = has_next(b), has_last(b)
                mask(b, 0)
                mask(b, 1)
                probs_out(b, 0)
                mask(b, 2)
                if last:
                    residual(b - 1)
                mask(b, 3)
                probs_out(b, 2)
                if nxt:
                    qkv_out(b + 1)
                mask(b, 4)
                mask(b, 5)
                probs_out(b, 4)
                if nxt:
                    rope_sum(b + 1)
                if last:
                    x1_rest(b - 1)
                mask(b, 6)
                mask(b, 7)
                probs_out(b, 6)
                if nxt:
                    keys_out(b + 1)
                normalize(b)

            dve.wait_ge(weights_in, 16 * len(weights))
            qkv_out(0)
            rope_sum(0)
            keys_out(0)
            slots(dve, slot)
            residual(B - 1)
            x1_rest(B - 1)

        @block.gpsimd
        def _(pool):
            def rope(a):
                pool.wait_ge(qkv_sb, a + 1)
                wait(pool, rope_done, a)
                qk = qkv[:, 0:NQK * D1].rearrange("p (h d) -> p h d", d=D1)
                half = D1 // 2
                pool.tensor_tensor(rope_a[:], qk, over(cos[:], NQK), ALU.mult)
                pool.tensor_tensor(rope_b[:, :, 0:half], qk[:, :, half:], over(sin[:, 0:half], NQK), ALU.mult)
                pool.tensor_tensor(rope_b[:, :, half:], qk[:, :, 0:half], over(sin[:, half:], NQK), ALU.mult).then_inc(rope_ab, 1)

            def values(a):
                pool.wait_ge(qkv_sb, a + 1)
                wait(pool, pv_done, 8 * a)
                hold(pool)
                pool.tensor_copy(v[:].rearrange("p g d -> p (g d)"), qkv[:, NQK * D1:]).then_inc(v_sb, 1)

            def with_bias(b):
                pool.wait_ge(xin_in, 16 * (b + 1))
                wait(pool, x1_sb, b)
                pool.tensor_tensor(xb[:], xin[:], b_dense[:], ALU.add).then_inc(xb_sb, 1)

            def slot(b):
                with_bias(b)
                if has_next(b):
                    rope(b + 1)
                    values(b + 1)

            pool.wait_ge(weights_in, 16 * len(weights))
            rope(0)
            values(0)
            slots(pool, slot)



def tables(nc, t, consts, x1t_unused=None):
    mask_row, mask_col, cw, sw = consts
    with ExitStack() as ctx:
        sb = lambda n, s, d=F32: ctx.enter_context(nc.sbuf_tensor("t_" + n, s, d))
        sem = lambda n: ctx.enter_context(nc.semaphore("t_" + n))
        lens = sb("lens", [P, B], I32)
        lenf = sb("lenf", [P, B])
        key_row = sb("key_row", [P, L])
        key_col = sb("key_col", [P, LT])
        token = sb("token", [P, 1])
        inv = sb("inv", [P, HD // 2])
        norms = sb("norms", [P, 2, HD])
        pos = sb("pos", [P, B])
        angle = sb("angle", [P, B, HD // 2])
        turns = sb("turns", [P, B, HD // 2])
        sine = sb("sine", [P, B, HD // 2])
        half_sine = sb("half_sine", [P, B, HD // 2])
        minus_sine = sb("minus_sine", [P, B, HD // 2])
        cosine = sb("cosine", [P, B, HD // 2])
        loaded, step, sines = sem("loaded"), sem("step"), sem("sines")
        block = ctx.enter_context(nc.Block())
        loads = ((lens, "lens"), (key_row, "key_row"), (key_col, "key_col"), (token, "token"), (inv, "inv"), (norms, "norms"))

        @block.sync
        def _(sp):
            for dst, name in loads:
                sp.dma_start(dst[:], t[name]).then_inc(loaded, 16)

        @block.vector
        def _(dve):
            done = [0]

            def then(op):
                done[0] += 1
                op.then_inc(step, 1)
                dve.wait_ge(step, done[0])

            dve.wait_ge(loaded, 16 * len(loads))
            then(dve.tensor_copy(lenf[:], lens[:]))
            then(dve.tensor_scalar(pos[:], lenf[:], token[:, 0:1], None, ALU.add))
            then(dve.tensor_tensor(angle[:], wide(pos[:], HD // 2), over(inv[:], B), ALU.mult))
            then(dve.tensor_scalar(turns[:], angle[:], 1.0 / (2 * np.pi), 12582912.0, ALU.mult, ALU.add))
            then(dve.tensor_scalar(turns[:], turns[:], 12582912.0, None, ALU.subtract))
            for part in TWO_PI:
                then(dve.scalar_tensor_tensor(out=angle[:], in0=turns[:], scalar=-part, in1=angle[:], op0=ALU.mult, op1=ALU.add))
            then(dve.tensor_scalar(angle[:], angle[:], 3.1415925, -3.1415925, ALU.min, ALU.max))
            dve.wait_ge(sines, 2)
            then(dve.tensor_tensor(cosine[:], half_sine[:], half_sine[:], ALU.mult))
            then(dve.tensor_scalar(cosine[:], cosine[:], -2.0, 1.0, ALU.mult, ALU.add))
            then(dve.tensor_scalar(minus_sine[:], sine[:], -1.0, None, ALU.mult))
            then(dve.tensor_scalar(norms[:, 0], norms[:, 0], SCALE2, None, ALU.mult))
            h = HD // 2
            for kind in range(2):
                lo, hi = norms[:, kind, 0:h], norms[:, kind, h:]
                dve.tensor_tensor(cw[:, :, kind, 0:h], cosine[:], over(lo, B), ALU.mult)
                dve.tensor_tensor(cw[:, :, kind, h:], cosine[:], over(hi, B), ALU.mult)
                dve.tensor_tensor(sw[:, :, kind, 0:h], minus_sine[:], over(hi, B), ALU.mult)
                dve.tensor_tensor(sw[:, :, kind, h:], sine[:], over(lo, B), ALU.mult)
            for b in range(B):
                dve.tensor_scalar(mask_row[:, b], key_row[:], lenf[:, b:b + 1], MASKED, ALU.is_ge, ALU.mult)
                dve.tensor_scalar(mask_col[:, b], key_col[:], lenf[:, b:b + 1], MASKED, ALU.is_ge, ALU.mult)

        @block.scalar
        def _(act):
            act.wait_ge(step, 9)
            act.activation(sine[:], angle[:], ACT.Sin).then_inc(sines, 1)
            act.activation(half_sine[:], angle[:], ACT.Sin, scale=0.5).then_inc(sines, 1)


def phase2_consts(nc, ctx):
    sb = lambda n, s, d: ctx.enter_context(nc.sbuf_tensor(n, s, d))
    return (sb("mask_row", [P, B, L], BF16), sb("mask_col", [P, B, LT], F32),
            sb("cw", [P, B, 2, HD], F32), sb("sw", [P, B, 2, HD], F32))


class Item:

    def __init__(self, g, b):
        self.g, self.b = (g, b) if b < B else (g + 1, b - B)
        self.n = self.g * B + self.b

    def ahead(self, k):
        return Item(self.g, self.b + k)

    def exists(self):
        return not (isinstance(self.g, int) and self.g >= G)


def phase2(nc, t, x1t_h, x1t_l, ident, consts, hacc, kv_dram):
    mask_row, mask_col, cw, sw = consts
    with ExitStack() as ctx:
        sb = lambda n, s, d=F32: ctx.enter_context(nc.sbuf_tensor("b_" + n, s, d))
        sem = lambda n: ctx.enter_context(nc.semaphore("b_" + n))
        ps = ctx.enter_context(nc.psum_tensor("b_ps", [P, 8, 512], F32))
        MX, ST, OT, SM, PJQ, PJK = (0, 1), (2, 3), 4, 5, 6, 7

        ones = sb("ones", [P, P])
        minus_ones = sb("minus_ones", [P, P], F32R)
        half = sb("half", [P, REP + 1])
        raw = sb("raw", [P, 2, QKV2])
        w_h, w_l = sb("w_h", [P, KT, QKV2], F32R), sb("w_l", [P, KT, QKV2], F32R)
        wo_h, wo_l = sb("wo_h", [P, REP, D], F32R), sb("wo_l", [P, REP, D], F32R)
        cache = sb("cache", [P, LT, 2 * HD])
        ss = sb("ss", [P, REP + 1])
        rstd = sb("rstd", [P, REP + 1])
        tq = sb("tq", [P, REP + 1, HD])
        ra = sb("ra", [P, REP + 1, HD])
        rb = sb("rb", [P, REP + 1, HD])
        qt_h, qt_l = sb("qt_h", [P, 2, REP * P], F32R), sb("qt_l", [P, 2, REP * P], F32R)
        kt_h, kt_l = sb("kt_h", [P, 2, NT * P], F32R), sb("kt_l", [P, 2, NT * P], F32R)
        v_h, v_l = sb("v_h", [P, 2, LT, HD], F32R), sb("v_l", [P, 2, LT, HD], F32R)
        vn_h, vn_l = sb("vn_h", [P, 4, HD], F32R), sb("vn_l", [P, 4, HD], F32R)
        unread = sb("unread", [P, 2, L], BF16)
        m_old, m_new, m_all = sb("m_old", [P, REP]), sb("m_new", [P, REP]), sb("m_all", [P, REP])
        diag = sb("diag", [P, REP, P], F32R)
        NP, NH = 2, 3
        NP, NH = 4, 4
        pf = sb("pf", [P, NP, REP * P])
        p_h, p_l = sb("p_h", [P, NH, REP * P], F32R), sb("p_l", [P, NH, REP * P], F32R)
        psum = sb("psum", [P, REP * P])
        rinv = sb("rinv", [P, REP * P])
        on = sb("on", [P, REP * P])
        o_h, o_l = sb("o_h", [P, REP * P], F32R), sb("o_l", [P, REP * P], F32R)

        const_sb = sem("const_sb")
        raw_in = [sem("raw_in0"), sem("raw_in1")]
        wh_sb, wl_sb, cache_in = sem("wh_sb"), sem("wl_sb"), sem("cache_in")
        k_ps, q_ps, kc_ps, qt_ps, kn_ps = sem("k_ps"), sem("q_ps"), sem("kc_ps"), sem("qt_ps"), sem("kn_ps")
        mx_ps, st_ps, pv_ps, sum_ps, wo_ps = sem("mx_ps"), sem("st_ps"), sem("pv_ps"), sem("sum_ps"), sem("wo_ps")
        vnh_sb, vnl_sb, sq_sb, tq_sb = sem("vnh_sb"), sem("vnl_sb"), sem("sq_sb"), sem("tq_sb")
        qth_sb, qtl_sb, kch_sb, kcl_sb = sem("qth_sb"), sem("qtl_sb"), sem("kch_sb"), sem("kcl_sb")
        knh_sb, knl_sb, vch_sb, vcl_sb = sem("knh_sb"), sem("knl_sb"), sem("vch_sb"), sem("vcl_sb")
        exp_sb, ph_sb, pl_sb, psum_sb = sem("exp_sb"), sem("ph_sb"), sem("pl_sb"), sem("psum_sb")
        ms_sb, rstd_sb, rab_sb, rope_sb = sem("ms_sb"), sem("rstd_sb"), sem("rab_sb"), sem("rope_sb")
        mx_sb, mall_sb, diag_sb = sem("mx_sb"), sem("mall_sb"), sem("diag_sb")
        rinv_sb, on_sb, oh_sb, ol_sb, h_sb = sem("rinv_sb"), sem("on_sb"), sem("oh_sb"), sem("ol_sb"), sem("h_sb")

        def slots(eng, slot):
            def head(g):
                for b in range(B):
                    slot(Item(g, b))
            head(0)
            with eng.Fori(1, G - 1) as g:
                head(g)
            head(G - 1)

        def flat(ap):
            return ap.rearrange("p a b -> p (a b)")

        block = ctx.enter_context(nc.Block())

        @block.sync
        def _(sp):
            def chunk(g, c):
                i = 8 * g + c
                wait(sp, wl_sb, i - 1)
                src = t["w2"][bass.ds(g, 1), c] if c < KT else t["wo2"][bass.ds(g, 1), c - KT]
                width = QKV2 if c < KT else D
                sp.dma_start(raw[:, c % 2, 0:width], src.rearrange("g p n -> (g p) n")).then_inc(raw_in[c % 2], 16)

            def rows(m):
                wait(sp, kc_ps, m.n)
                wait(sp, vcl_sb, m.n)
                src = kv_dram[m.b, bass.ds(m.g, 1)].rearrange("g (t p) d -> p (g t) d", p=P)
                sp.dma_start(cache[:], src).then_inc(cache_in, 16)

            def slot(m):
                if m.ahead(2).exists():
                    rows(m.ahead(2))
                if m.b == 0:
                    for c in range(KT, 2 * KT):
                        chunk(m.g, c)
                if m.b == 5 and m.ahead(3).exists():
                    for c in range(KT):
                        chunk(m.g + 1, c)

            for c in range(KT):
                chunk(0, c)
            rows(Item(0, 0))
            rows(Item(0, 1))
            slots(sp, slot)

        @block.tensor
        def _(pe):
            def three(out, lhs, rhs, start=True, stop=True):
                pe.matmul(out, lhs[0], rhs[0], start=start, stop=False)
                pe.matmul(out, lhs[0], rhs[1], start=False, stop=False)
                return pe.matmul(out, lhs[1], rhs[0], start=False, stop=stop)

            def project(m, bank, cols, done):
                pe.wait_ge(wl_sb, 8 * m.g + KT)
                for k in range(KT):
                    mm = three(ps[:, bank, 0:cols.stop - cols.start], (x1t_h[:, m.b, k], x1t_l[:, m.b, k]),
                               (w_h[:, k, cols], w_l[:, k, cols]), k == 0, k == KT - 1)
                mm.then_inc(done, 1)

            def project_kv(m):
                wait(pe, knl_sb, m.n)
                project(m, PJK, slice(REP * HD, QKV2), k_ps)

            def project_q(m):
                wait(pe, qtl_sb, m.n)
                project(m, PJQ, slice(0, REP * HD), q_ps)

            def turn_cache(m):
                pe.wait_ge(cache_in, 16 * (m.n + 1))
                pe.wait_ge(tq_sb, m.n + 1)
                pe.wait_ge(vnl_sb, m.n + 1)
                for i in range(LT):
                    mm = pe.transpose(ps[:, PJK, i * P:(i + 1) * P], cache[:, i, 0:HD], ident[:])
                mm.then_inc(kc_ps, 1)

            def turn_q(m):
                pe.wait_ge(rope_sb, m.n + 1)
                for h in range(REP):
                    mm = pe.transpose(ps[:, PJQ, h * P:(h + 1) * P], ra[:, h], ident[:])
                mm.then_inc(qt_ps, 1)

            def turn_new(m):
                pe.wait_ge(kcl_sb, m.n + 1)
                pe.transpose(ps[:, PJK, 0:P], ra[:, REP], ident[:]).then_inc(kn_ps, 1)

            def row_scores(m, i):
                k = m.b % 2
                bank = MX[(NT * m.b + i) % 2]
                if i == 0:
                    pe.wait_ge(qth_sb, m.n + 1)
                    pe.wait_ge(knh_sb, m.n + 1)
                wait(pe, mx_sb, NT * m.n + i - 1)
                if i < REP:
                    mm = pe.matmul(ps[:, bank, :], qt_h[:, k, i * P:(i + 1) * P], kt_h[:, k, 0:L], start=True, stop=True)
                else:
                    for h in range(REP):
                        mm = pe.matmul(ps[:, bank, h * P:(h + 1) * P], qt_h[:, k, h * P:(h + 1) * P], kt_h[:, k, L:],
                                       start=True, stop=True)
                mm.then_inc(mx_ps, 1)

            def scores(m, i):
                k = m.b % 2
                bank = ps[:, ST[(NT * m.b + i) % 2], :]
                if i == 0:
                    pe.wait_ge(diag_sb, m.n + 1)
                    pe.wait_ge(qtl_sb, m.n + 1)
                    pe.wait_ge(knl_sb, m.n + 1)
                wait(pe, exp_sb, NT * m.n + i - 1)
                pe.matmul(bank, minus_ones[:], flat(diag[:]), start=True, stop=False)
                tile = slice(i * P, (i + 1) * P)
                three(bank, (kt_h[:, k, tile], kt_l[:, k, tile]), (qt_h[:, k], qt_l[:, k]), False).then_inc(st_ps, 1)

            def values(m, i):
                k, j = m.b % 2, (NT * m.b + i) % NH
                if i == 0:
                    wait(pe, on_sb, m.n)
                    pe.wait_ge(vcl_sb, m.n + 1)
                pe.wait_ge(pl_sb, NT * m.n + i + 1)
                v = (v_h[:, k, i], v_l[:, k, i]) if i < LT else (vn_h[:, m.b % 4], vn_l[:, m.b % 4])
                three(ps[:, OT, :], v, (p_h[:, j], p_l[:, j]), i == 0, i == LT).then_inc(pv_ps, 1)

            def sums(m):
                pe.wait_ge(psum_sb, LT * (m.n + 1))
                wait(pe, h_sb, m.n)
                pe.matmul(ps[:, SM, :], ones[:], psum[:], start=True, stop=True).then_inc(sum_ps, 1)

            def out_product(m):
                pe.wait_ge(ol_sb, m.n + 1)
                pe.wait_ge(wl_sb, 8 * (m.g + 1))
                for h in range(REP):
                    tile = slice(h * P, (h + 1) * P)
                    mm = three(ps[:, SM, :], (o_h[:, tile], o_l[:, tile]), (wo_h[:, h], wo_l[:, h]), h == 0, h == REP - 1)
                mm.then_inc(wo_ps, 1)

            def slot(m):
                one, two = m.ahead(1), m.ahead(2)
                scores(m, 0)
                if one.exists():
                    turn_cache(one)
                scores(m, 1)
                if not (isinstance(m.n, int) and m.n == 0):
                    out_product(Item(m.g, m.b - 1) if m.b else Item(m.g - 1, B - 1))
                scores(m, 2)
                values(m, 0)
                if one.exists():
                    turn_q(one)
                    turn_new(one)
                scores(m, 3)
                values(m, 1)
                if two.exists():
                    project_kv(two)
                if one.exists():
                    row_scores(one, 0)
                    row_scores(one, 1)
                scores(m, 4)
                values(m, 2)
                if two.exists():
                    project_q(two)
                if one.exists():
                    row_scores(one, 2)
                    row_scores(one, 3)
                values(m, 3)
                if one.exists():
                    row_scores(one, 4)
                values(m, 4)
                sums(m)

            pe.wait_ge(const_sb, 4)
            zero, one = Item(0, 0), Item(0, 1)
            project_kv(zero)
            project_q(zero)
            turn_cache(zero)
            turn_q(zero)
            turn_new(zero)
            project_kv(one)
            for i in range(NT):
                row_scores(zero, i)
            project_q(one)
            slots(pe, slot)
            out_product(Item(G - 1, B - 1))

        @block.scalar
        def _(act):
            def weights(g, cs):
                for c in cs:
                    i = 8 * g + c
                    act.wait_ge(raw_in[c % 2], 16 * (4 * g + c // 2 + 1))
                    if c == 0:
                        wait(act, q_ps, 8 * g)
                    if c == KT:
                        wait(act, wo_ps, 8 * g)
                    dst = w_h[:, c] if c < KT else wo_h[:, c - KT]
                    act.activation(dst, raw[:, c % 2, 0:QKV2 if c < KT else D], ACT.Copy).then_inc(wh_sb, 1)

            def new_kv(m):
                act.wait_ge(k_ps, m.n + 1)
                wait(act, rstd_sb, m.n)
                wait(act, rab_sb, m.n)
                act.activation(tq[:, REP], ps[:, PJK, 0:HD], ACT.Square, accum_out=ss[:, REP:REP + 1])
                wait(act, pv_ps, NT * (m.n - 3))
                act.activation(vn_h[:, m.b % 4], ps[:, PJK, HD:2 * HD], ACT.Copy).then_inc(vnh_sb, 1)

            def squares(m):
                act.wait_ge(q_ps, m.n + 1)
                for h in range(REP):
                    op = act.activation(tq[:, h], ps[:, PJQ, h * P:(h + 1) * P], ACT.Square, accum_out=ss[:, h:h + 1])
                op.then_inc(sq_sb, 1)

            def normalize(m):
                act.wait_ge(rstd_sb, m.n + 1)
                act.wait_ge(vnl_sb, m.n + 1)
                act.activation(tq[:, REP], ps[:, PJK, 0:HD], ACT.Copy, scale=rstd[:, REP:REP + 1])
                for h in range(REP):
                    op = act.activation(tq[:, h], ps[:, PJQ, h * P:(h + 1) * P], ACT.Copy, scale=rstd[:, h:h + 1])
                op.then_inc(tq_sb, 1)

            def cache_keys(m):
                act.wait_ge(kc_ps, m.n + 1)
                wait(act, st_ps, NT * (m.n - 1))
                act.activation(kt_h[:, m.b % 2, 0:L], ps[:, PJK, :], ACT.Copy).then_inc(kch_sb, 1)

            def cache_values(m):
                act.wait_ge(cache_in, 16 * (m.n + 1))
                wait(act, pv_ps, NT * (m.n - 1))
                act.activation(v_h[:, m.b % 2], cache[:, :, HD:], ACT.Copy).then_inc(vch_sb, 1)

            def queries(m):
                act.wait_ge(qt_ps, m.n + 1)
                act.activation(qt_h[:, m.b % 2], ps[:, PJQ, :], ACT.Copy).then_inc(qth_sb, 1)

            def new_keys(m):
                act.wait_ge(kn_ps, m.n + 1)
                act.activation(kt_h[:, m.b % 2, L:], ps[:, PJK, 0:P], ACT.Copy).then_inc(knh_sb, 1)

            def exponent(m, i):
                s = NT * m.b + i
                act.wait_ge(st_ps, NT * m.n + i + 1)
                wait(act, pl_sb, NT * m.n + i + 1 - NP)
                before = LT * m.n + i if i == 4 else LT * (m.n - 1) + i + 1
                before = LT * m.n + 1 if i == 4 else before
                wait(act, psum_sb, before)
                bias = mask_col[:, m.b, i:i + 1] if i < LT else 0.0
                act.activation(pf[:, s % NP], ps[:, ST[s % 2], :], ACT.Exp, bias=bias).then_inc(exp_sb, 1)

            def high(m, i):
                s = NT * m.b + i
                act.wait_ge(exp_sb, NT * m.n + i + 1)
                wait(act, pv_ps, NT * m.n + i + 1 - NH)
                act.activation(p_h[:, s % NH], pf[:, s % NP], ACT.Copy).then_inc(ph_sb, 1)

            def output(m):
                act.wait_ge(on_sb, m.n + 1)
                wait(act, wo_ps, m.n)
                act.activation(o_h[:], on[:], ACT.Copy).then_inc(oh_sb, 1)

            def slot(m):
                one, two = m.ahead(1), m.ahead(2)
                exponent(m, 0)
                if not (isinstance(m.n, int) and m.n == 0):
                    output(Item(m.g, m.b - 1) if m.b else Item(m.g - 1, B - 1))
                if one.exists():
                    cache_keys(one)
                high(m, 0)
                exponent(m, 1)
                high(m, 1)
                if m.b == 6 and two.exists():
                    weights(m.g + 1, range(KT))
                exponent(m, 2)
                if one.exists():
                    cache_values(one)
                high(m, 2)
                if one.exists():
                    queries(one)
                    new_keys(one)
                if m.b == 0:
                    weights(m.g, range(KT, 2 * KT))
                exponent(m, 3)
                high(m, 3)
                if two.exists():
                    new_kv(two)
                exponent(m, 4)
                high(m, 4)
                if two.exists():
                    squares(two)
                    normalize(two)

            zero, one = Item(0, 0), Item(0, 1)
            weights(0, range(KT))
            new_kv(zero)
            squares(zero)
            normalize(zero)
            cache_keys(zero)
            cache_values(zero)
            queries(zero)
            new_keys(zero)
            new_kv(one)
            squares(one)
            normalize(one)
            slots(act, slot)
            output(Item(G - 1, B - 1))

        @block.vector
        def _(dve):
            def weights(g, cs):
                for c in cs:
                    dve.wait_ge(wh_sb, 8 * g + c + 1)
                    width = QKV2 if c < KT else D
                    h, l = (w_h[:, c], w_l[:, c]) if c < KT else (wo_h[:, c - KT], wo_l[:, c - KT])
                    dve.tensor_tensor(l, raw[:, c % 2, 0:width], h, ALU.subtract).then_inc(wl_sb, 1)

            def new_values(m):
                dve.wait_ge(vnh_sb, m.n + 1)
                dve.tensor_tensor(vn_l[:, m.b % 4], ps[:, PJK, HD:2 * HD], vn_h[:, m.b % 4], ALU.subtract).then_inc(vnl_sb, 1)

            def cache_keys(m):
                dve.wait_ge(kch_sb, m.n + 1)
                dve.tensor_tensor(kt_l[:, m.b % 2, 0:L], ps[:, PJK, :], kt_h[:, m.b % 2, 0:L], ALU.subtract).then_inc(kcl_sb, 1)

            def rope(m):
                dve.wait_ge(rab_sb, m.n + 1)
                dve.tensor_tensor(ra[:], ra[:], rb[:], ALU.add).then_inc(rope_sb, 1)

            def queries(m):
                dve.wait_ge(qth_sb, m.n + 1)
                dve.tensor_tensor(qt_l[:, m.b % 2], ps[:, PJQ, :], qt_h[:, m.b % 2], ALU.subtract).then_inc(qtl_sb, 1)

            def new_keys(m):
                dve.wait_ge(knh_sb, m.n + 1)
                dve.tensor_tensor(kt_l[:, m.b % 2, L:], ps[:, PJK, 0:P], kt_h[:, m.b % 2, L:], ALU.subtract).then_inc(knl_sb, 1)

            def maxima(m, i):
                s = NT * m.b + i
                dve.wait_ge(mx_ps, NT * m.n + i + 1)
                bank = MX[s % 2]
                if i < REP:
                    wait(dve, mx_sb, NT * m.n + i - (1 if i else 2))
                    hold(dve)
                    dve.tensor_tensor_reduce(unread[:, i % 2], ps[:, bank, :], mask_row[:, m.b], 1.0, MASKED, ALU.add, ALU.max,
                                             m_old[:, i:i + 1]).then_inc(mx_sb, 1)
                else:
                    dve.tensor_reduce(m_new[:], ps[:, bank, :].rearrange("p (h s) -> p h s", h=REP), AX.X, ALU.max).then_inc(mx_sb, 1)

            def diagonal(m):
                dve.wait_ge(mx_sb, NT * (m.n + 1))
                dve.tensor_tensor(m_all[:], m_old[:], m_new[:], ALU.max).then_inc(mall_sb, 1)
                dve.wait_ge(mall_sb, m.n + 1)
                wait(dve, st_ps, NT * m.n)
                dve.tensor_tensor(diag[:], over(ident[:], REP), wide(m_all[:], P), ALU.mult).then_inc(diag_sb, 1)

            def low(m, i):
                s = NT * m.b + i
                dve.wait_ge(ph_sb, NT * m.n + i + 1)
                dve.tensor_tensor(p_l[:, s % NH], pf[:, s % NP], p_h[:, s % NH], ALU.subtract).then_inc(pl_sb, 1)

            def normalize(m):
                dve.wait_ge(sum_ps, m.n + 1)
                dve.reciprocal(rinv[:], ps[:, SM, :]).then_inc(rinv_sb, 1)
                dve.wait_ge(rinv_sb, m.n + 1)
                dve.wait_ge(pv_ps, NT * (m.n + 1))
                wait(dve, oh_sb, m.n)
                wait(dve, ol_sb, m.n)
                dve.tensor_tensor(on[:], ps[:, OT, :], rinv[:], ALU.mult).then_inc(on_sb, 1)

            def output(m):
                dve.wait_ge(oh_sb, m.n + 1)
                dve.tensor_tensor(o_l[:], on[:], o_h[:], ALU.subtract).then_inc(ol_sb, 1)

            def accumulate(m):
                dve.wait_ge(wo_ps, m.n + 1)
                if not isinstance(m.n, int) or m.n:
                    wait(dve, h_sb, m.n)
                else:
                    dve.wait_ge(const_sb, 3)
                dve.tensor_tensor(hacc[:, m.b], ps[:, SM, :], hacc[:, m.b], ALU.add).then_inc(h_sb, 1)

            def slot(m):
                one, two = m.ahead(1), m.ahead(2)
                last = None if isinstance(m.n, int) and m.n == 0 else Item(m.g, m.b - 1) if m.b else Item(m.g - 1, B - 1)
                if last:
                    normalize(last)
                if one.exists():
                    cache_keys(one)
                if last:
                    output(last)
                low(m, 0)
                if one.exists():
                    rope(one)
                low(m, 1)
                if last:
                    accumulate(last)
                if m.b == 6 and two.exists():
                    weights(m.g + 1, range(KT))
                low(m, 2)
                if one.exists():
                    queries(one)
                    new_keys(one)
                if m.b == 0:
                    weights(m.g, range(KT, 2 * KT))
                low(m, 3)
                if two.exists():
                    new_values(two)
                if one.exists():
                    maxima(one, 0)
                    maxima(one, 1)
                low(m, 4)
                if one.exists():
                    for i in range(2, NT):
                        maxima(one, i)
                    diagonal(one)

            dve.memset(ones[:], 1.0).then_inc(const_sb, 1)
            dve.memset(hacc[:], 0.0).then_inc(const_sb, 1)
            dve.memset(minus_ones[:].bitcast(F32), -1.0).then_inc(const_sb, 1)
            zero, one = Item(0, 0), Item(0, 1)
            weights(0, range(KT))
            new_values(zero)
            cache_keys(zero)
            rope(zero)
            queries(zero)
            new_keys(zero)
            new_values(one)
            for i in range(NT):
                maxima(zero, i)
            diagonal(zero)
            slots(dve, slot)
            last = Item(G - 1, B - 1)
            normalize(last)
            output(last)
            accumulate(last)

        @block.gpsimd
        def _(pool):
            def rms(m):
                pool.wait_ge(sq_sb, m.n + 1)
                wait(pool, tq_sb, m.n)
                hold(pool)
                pool.tensor_scalar(rstd[:], ss[:], 1.0 / HD, EPS, ALU.mult, ALU.add).then_inc(ms_sb, 1)
                pool.wait_ge(ms_sb, m.n + 1)
                pool.tensor_tensor(rstd[:], rstd[:], half[:], ALU.pow).then_inc(rstd_sb, 1)

            def rope(m):
                pool.wait_ge(tq_sb, m.n + 1)
                wait(pool, kn_ps, m.n)
                wait(pool, rope_sb, m.n)
                h = HD // 2
                for x, kind in ((slice(0, REP), 0), (slice(REP, REP + 1), 1)):
                    n = x.stop - x.start
                    pool.tensor_tensor(ra[:, x], tq[:, x], over(cw[:, m.b, kind], n), ALU.mult)
                    pool.tensor_tensor(rb[:, x, 0:h], tq[:, x, h:], over(sw[:, m.b, kind, 0:h], n), ALU.mult)
                    op = pool.tensor_tensor(rb[:, x, h:], tq[:, x, 0:h], over(sw[:, m.b, kind, h:], n), ALU.mult)
                op.then_inc(rab_sb, 1)

            def cache_values(m):
                pool.wait_ge(vch_sb, m.n + 1)
                pool.tensor_tensor(v_l[:, m.b % 2], cache[:, :, HD:], v_h[:, m.b % 2], ALU.subtract).then_inc(vcl_sb, 1)

            def add(m, i):
                s = NT * m.b + i
                pool.wait_ge(exp_sb, NT * m.n + i + 1)
                if i == 1:
                    wait(pool, sum_ps, m.n)
                    first = pf[:, (s - 1) % NP]
                else:
                    pool.wait_ge(psum_sb, LT * m.n + i - 1)
                    first = psum[:]
                pool.tensor_tensor(psum[:], first, pf[:, s % NP], ALU.add).then_inc(psum_sb, 1)

            def slot(m):
                one, two = m.ahead(1), m.ahead(2)
                add(m, 1)
                add(m, 2)
                if one.exists():
                    cache_values(one)
                add(m, 3)
                add(m, 4)
                if two.exists():
                    rms(two)
                    rope(two)

            pool.memset(half[:], -0.5).then_inc(const_sb, 1)
            pool.wait_ge(const_sb, 4)
            zero, one = Item(0, 0), Item(0, 1)
            rms(zero)
            rope(zero)
            cache_values(zero)
            rms(one)
            rope(one)
            slots(pool, slot)


def phase3(nc, t, ident, hacc, x1_dram, out):
    with ExitStack() as ctx:
        sb = lambda n, s, d=F32: ctx.enter_context(nc.sbuf_tensor("c_" + n, s, d))
        sem = lambda n: ctx.enter_context(nc.semaphore("c_" + n))
        ps = ctx.enter_context(nc.psum_tensor("c_ps", [P, 8, 512], F32))
        HT, F, GL, LO = (0, 1), (2, 3), (4, 5), (6, 7)
        NX = NR + MAXR

        wf = sb("wf", [P, KT, D])
        wx = sb("wx", [P, KT, NX])
        bt = sb("bt", [MAXR, D])
        b_ffn = sb("b_ffn", [P, D])
        b_gate = sb("b_gate", [P, NR])
        first = sb("first", [P, NR])
        most = sb("most", [P, MAXR])
        x1 = sb("x1", [P, B, D])
        ht = sb("ht", [P, 2, KT, P])
        sc = sb("sc", [P, 2, NR])
        top = sb("top", [P, 2])
        weight = sb("weight", [P, 2, NR])
        expert = sb("expert", [P, 2])
        low = sb("low", [P, 2, MAXR])
        lowt = sb("lowt", [MAXR, 2, P])
        y = sb("y", [P, 2, D])

        weights_in, x1_in, stored = sem("weights_in"), sem("x1_in"), [sem("stored0"), sem("stored1")]
        ht_ps, ht_sb, gl_ps, f_ps = sem("ht_ps"), sem("ht_sb"), sem("gl_ps"), sem("f_ps")
        sc_sb, top_sb, weight_sb = sem("sc_sb"), sem("top_sb"), sem("weight_sb")
        expert_sb, low_sb = sem("expert_sb"), sem("low_sb")
        lowt_ps, lowt_sb, xb_sb, y_sb = sem("lowt_ps"), sem("lowt_sb"), sem("xb_sb"), sem("y_sb")
        block = ctx.enter_context(nc.Block())
        weights = ((wx, "wx"), (wf, "wf"), (bt, "bt"), (b_gate, "b_gate"), (first, "first"), (most, "most"), (b_ffn, "b_ffn"))

        @block.sync
        def _(sp):
            for dst, name in weights:
                sp.dma_start(dst[:], t[name]).then_inc(weights_in, 16)
            sp.dma_start(x1[:], x1_dram.rearrange("b s d -> s b d")).then_inc(x1_in, 16)
            for b in range(B):
                sp.wait_ge(y_sb, b + 1)
                sp.dma_start(out[b], y[:, b % 2]).then_inc(stored[b % 2], 16)
            for k in range(2):
                sp.wait_ge(stored[k], 16 * (B // 2))

        @block.tensor
        def _(pe):
            def turn(b):
                wait(pe, ht_sb, b - 1)
                for i in range(KT):
                    mm = pe.transpose(ps[:, HT[b % 2], i * P:(i + 1) * P], hacc[:, b, i * P:(i + 1) * P], ident[:])
                mm.then_inc(ht_ps, 1)

            pe.wait_ge(weights_in, 16 * len(weights))
            turn(0)
            for b in range(B):
                k = b % 2
                pe.wait_ge(ht_sb, b + 1)
                wait(pe, low_sb, b - 1)
                for i in range(KT):
                    mm = pe.matmul(ps[:, GL[k], 0:NX], ht[:, k, i], wx[:, i], start=i == 0, stop=i == KT - 1)
                mm.then_inc(gl_ps, 1)
                if b + 1 < B:
                    turn(b + 1)
                wait(pe, y_sb, b - 1)
                for i in range(KT):
                    pe.matmul(ps[:, F[k], :], ht[:, k, i], wf[:, i], start=i == 0, stop=False)
                pe.wait_ge(low_sb, b + 1)
                wait(pe, lowt_sb, b - 1)
                pe.transpose(ps[0:MAXR, LO[k], 0:P], low[:, k], ident[:]).then_inc(lowt_ps, 1)
                pe.wait_ge(lowt_sb, b + 1)
                pe.matmul(ps[:, F[k], :], lowt[:, k], bt[:], start=False, stop=True).then_inc(f_ps, 1)

        @block.scalar
        def _(act):
            def h_out(b):
                act.wait_ge(ht_ps, b + 1)
                wait(act, f_ps, b - 1)
                act.activation(ht[:, b % 2].rearrange("p k s -> p (k s)"), ps[:, HT[b % 2], :], ACT.Copy).then_inc(ht_sb, 1)

            h_out(0)
            for b in range(B):
                if b + 1 < B:
                    h_out(b + 1)
                act.wait_ge(lowt_ps, b + 1)
                act.activation(lowt[:, b % 2], ps[0:MAXR, LO[b % 2], 0:P], ACT.Copy).then_inc(lowt_sb, 1)

        @block.vector
        def _(dve):
            dve.wait_ge(weights_in, 16 * len(weights))
            for b in range(B):
                k = b % 2
                dve.wait_ge(gl_ps, b + 1)
                dve.tensor_tensor(sc[:, k], ps[:, GL[k], 0:NR], b_gate[:], ALU.add).then_inc(sc_sb, 1)
                dve.wait_ge(sc_sb, b + 1)
                dve.tensor_reduce(top[:, k:k + 1], sc[:, k], AX.X, ALU.max).then_inc(top_sb, 1)
                dve.wait_ge(top_sb, b + 1)
                dve.scalar_tensor_tensor(out=weight[:, k], in0=sc[:, k], scalar=top[:, k:k + 1], in1=first[:],
                                         op0=ALU.is_ge, op1=ALU.mult).then_inc(weight_sb, 1)
                dve.wait_ge(weight_sb, b + 1)
                dve.tensor_reduce(expert[:, k:k + 1], weight[:, k], AX.X, ALU.max).then_inc(expert_sb, 1)
                dve.wait_ge(expert_sb, b + 1)
                wait(dve, lowt_ps, b - 1)
                dve.scalar_tensor_tensor(out=low[:, k], in0=most[:], scalar=expert[:, k:k + 1], in1=ps[:, GL[k], NR:NX],
                                         op0=ALU.is_ge, op1=ALU.mult).then_inc(low_sb, 1)
                dve.wait_ge(f_ps, b + 1)
                dve.wait_ge(xb_sb, b + 1)
                wait(dve, stored[k], 16 * (b // 2))
                dve.tensor_tensor(y[:, k], ps[:, F[k], :], x1[:, b], ALU.add).then_inc(y_sb, 1)

        @block.gpsimd
        def _(pool):
            pool.wait_ge(weights_in, 16 * len(weights))
            pool.wait_ge(x1_in, 16)
            for b in range(B):
                pool.tensor_tensor(x1[:, b], x1[:, b], b_ffn[:], ALU.add).then_inc(xb_sb, 1)


def build_program(nc, t, out):
    x1_dram = nc.dram_tensor("x1", [B, S, D], F32).ap()
    kv_dram = nc.dram_tensor("kv_of_batch", [B, G, L, 2 * HD], F32).ap()
    with ExitStack() as ctx:
        sb = lambda n, s, d=F32: ctx.enter_context(nc.sbuf_tensor(n, s, d))
        ident = sb("ident", [P, P])
        hacc = sb("hacc", [P, B, D])
        with ExitStack() as inner:
            sb2 = lambda n, s, d: inner.enter_context(nc.sbuf_tensor(n, s, d))
            x1t_h = sb2("x1t_h", [P, B, KT, P], F32R)
            x1t_l = sb2("x1t_l", [P, B, KT, P], F32R)
            phase1(nc, t, x1t_h, x1t_l, ident, x1_dram, kv_dram)
            consts = phase2_consts(nc, inner)
            tables(nc, t, consts)
            phase2(nc, t, x1t_h, x1t_l, ident, consts, hacc, kv_dram)
        phase3(nc, t, ident, hacc, x1_dram, out)


def host_arrays(**i):
    f = lambda a: np.ascontiguousarray(a)
    arange = lambda n: np.arange(n, dtype=np.float32)
    t = {}
    t["x"] = f(i["x"])
    t["xt"] = f(i["x"].reshape(B, S, KT, P).transpose(3, 2, 0, 1))
    rows = lambda w: f(w.T.reshape(KT, P, w.shape[0]).transpose(1, 0, 2))
    t["wc"] = rows(i["L0_cond_weight"])
    t["b_cond"] = f(i["L0_cond_bias"].reshape(KT, P).T)
    t["la"] = f(i["L0_cond_lora_a_weights"].transpose(0, 2, 1))
    t["lb"] = f(i["L0_cond_lora_b_weights"].transpose(0, 2, 1))
    t["ls"] = f(np.broadcast_to(i["L0_cond_scaling_factors"].reshape(8, 1, 1), (8, R1, 1)))
    t["adapters"] = f(i["itok_B_1_7"].reshape(1, B))
    t["pages"] = f(i["itok_Bx16_0_63"].reshape(1, B * NPP))

    def by_kind(w):
        w = w.reshape(G1, 6, D1, *w.shape[1:])
        return np.concatenate([w[:, 0:4].reshape(H1 * D1, *w.shape[3:]), w[:, 4].reshape(G1 * D1, *w.shape[3:]),
                               w[:, 5].reshape(G1 * D1, *w.shape[3:])])

    t["wq"] = rows(by_kind(i["L0_attn_w_qkv"]))
    t["b_qkv"] = f(np.broadcast_to(by_kind(i["L0_attn_b_qkv"]), (P, QKV1)))
    t["wd"] = rows(i["L0_attn_w_dense"])
    t["b_dense"] = f(np.broadcast_to(i["L0_attn_b_dense"], (P, D)))
    freqs = np.outer(arange(S), np.float32(1.0) / np.float32(1000000.0) ** (np.arange(0, D1, 2, dtype=np.float32) / np.float32(D1)))
    t["cos"] = f(np.concatenate([np.cos(freqs), np.cos(freqs)], 1).astype(np.float32))
    t["sin"] = f(np.concatenate([-np.sin(freqs), np.sin(freqs)], 1).astype(np.float32))
    t["causal"] = np.where(np.tri(S, dtype=bool), np.float32(0), np.float32(MASKED))
    t["blocks"] = np.kron(np.eye(8, dtype=np.float32), np.ones((D1, 1), np.float32))
    t["ident"] = np.eye(P, dtype=np.float32)
    heads = lambda w, n: w.reshape(G, n * HD, D)
    w2 = np.concatenate([heads(i["L0_cond2_Wq"], REP), heads(i["L0_cond2_Wk"], 1), heads(i["L0_cond2_Wv"], 1)], 1)
    t["w2"] = f(w2.transpose(0, 2, 1).reshape(G, KT, P, QKV2))
    t["wo2"] = f(i["L0_cond2_Wo"].T.reshape(G, REP, HD, D))
    t["lens"] = f(np.broadcast_to(i["itok_B_207_1644"], (P, B)))
    t["key_row"] = f(np.broadcast_to(arange(L), (P, L)))
    t["key_col"] = f(arange(L).reshape(LT, P).T)
    t["token"] = arange(S).reshape(P, 1)
    t["inv"] = f(np.broadcast_to(np.float32(1.0) / np.float32(10000.0) ** (np.arange(0, HD, 2, dtype=np.float32) / np.float32(HD)), (P, HD // 2)))
    t["norms"] = f(np.broadcast_to(np.stack([i["L0_cond2_q_norm_w"], i["L0_cond2_k_norm_w"]]), (P, 2, HD)))
    t["wf"] = rows(i["L0_ffn_W"])
    t["wx"] = rows(np.concatenate([i["L0_ffn_gate_w"], i["L0_ffn_A"]]))
    t["bt"] = f(i["L0_ffn_B"].T)
    t["b_ffn"] = f(np.broadcast_to(i["L0_ffn_b"], (P, D)))
    t["b_gate"] = f(np.broadcast_to(i["L0_ffn_gate_b"], (P, NR)))
    t["first"] = f(np.broadcast_to(NR - arange(NR), (P, NR)))
    keeps = np.array([NR - min(j for j in range(NR) if RANKS[j] > r) for r in range(MAXR)], np.float32)
    t["most"] = f(np.broadcast_to(keeps, (P, MAXR)))
    t["kv"] = f(np.concatenate([i["L0_cond2_k_cache"], i["L0_cond2_v_cache"]], -1).transpose(0, 2, 1, 3))
    return t



def kernel(**inputs):
    import concourse.bacc as bacc
    from concourse.bass_utils import run_bass_kernel_spmd

    nc = bacc.Bacc("TRN2", target_bir_lowering=False, num_devices=1)
    arrays = host_arrays(**{name: np.asarray(a) for name, a in inputs.items()})
    t = {name: nc.dram_tensor(f"in_{name}", a.shape, mybir.dt.from_np(a.dtype), kind="ExternalInput").ap()
         for name, a in arrays.items()}
    out = nc.dram_tensor("out", [B, S, D], F32, kind="ExternalOutput").ap()
    build_program(nc, t, out)
    got = run_bass_kernel_spmd(nc, [{f"in_{name}": a for name, a in arrays.items()}], core_ids=[0])
    return got.results[0]["out"]
```

```python
from contextlib import ExitStack

import numpy as np

import concourse.bass as bass
from concourse import mybir

ALU = mybir.AluOpType
ACT = mybir.ActivationFunctionType
AX = mybir.AxisListType
F32 = mybir.dt.float32
F32R = mybir.dt.float32r
BF16 = mybir.dt.bfloat16
I32 = mybir.dt.int32

P = 128
B, S, D = 8, 128, 512
KT = D // P
H1, G1, D1 = 32, 8, 16
R1 = 16
C1 = 8
QKV1 = (H1 + 2 * G1) * D1
G, REP, HD = 8, 4, 128
PAGES, PSIZE, NPP = 64, 32, 16
L = PSIZE * NPP
LT = L // P
NT = LT + 1
QKV2 = (REP + 2) * HD
SCALE2 = 1.0 / float(np.sqrt(HD))
EPS = 1e-6
MASKED = -1e30
TWO_PI = (6.28125, 0.0019350051879882812, 3.019916050e-07)
RANKS = (8, 16, 32, 64)
MAXR, NR = 64, 4
W3 = D + NR + MAXR


def wait(eng, sem, value):
    if isinstance(value, int) and value <= 0:
        return
    eng.wait_ge(sem, value)


def hold(eng):
    eng.nop(nofuse=True)


def wide(ap, n):
    return ap.unsqueeze(2).broadcast_to([ap.shape[0], ap.shape[1], n])


def over(ap, n):
    return ap.unsqueeze(1).broadcast_to([ap.shape[0], n, ap.shape[1]])


def phase1(nc, t, x1t_h, x1t_l, ident, consts, raw, raw_in, x1_dram, kv_dram):
    with ExitStack() as ctx:
        sb = lambda n, s, d=F32: ctx.enter_context(nc.sbuf_tensor("a_" + n, s, d))
        sem = lambda n: ctx.enter_context(nc.semaphore("a_" + n))
        ps = ctx.enter_context(nc.psum_tensor("a_ps", [P, 8, 512], F32))
        SC, PT, CTX, M0, M1, M2 = (0, 1), (2, 3), 4, 5, 6, 7
        NQK = H1 + G1

        wc = sb("wc", [P, KT, D])
        wq = sb("wq", [P, KT, QKV1])
        wd = sb("wd", [P, KT, D])
        b_cond = sb("b_cond", [P, KT])
        b_qkv = sb("b_qkv", [P, QKV1])
        b_dense = sb("b_dense", [P, D])
        cos = sb("cos", [P, D1])
        sin = sb("sin", [P, D1])
        causal = sb("causal", [P, P])
        blocks = sb("blocks", [P, 8])
        adapters = sb("adapters", [1, B], I32)
        pages = sb("pages", [1, B * NPP], I32)
        la = sb("la", [P, KT, R1])
        lb = sb("lb", [R1, D])
        ls = sb("ls", [R1, 1])
        xt = sb("xt", [P, KT, P])
        xin = sb("xin", [P, D])
        low = sb("low", [R1, P])
        yt = sb("yt", [P, KT, P])
        qkv = sb("qkv", [P, QKV1])
        rope_a = sb("rope_a", [P, NQK, D1])
        rope_b = sb("rope_b", [P, NQK, D1])
        qr = sb("qr", [P, D])
        kr = sb("kr", [P, G1, 4, D1])
        v = sb("v", [P, G1, D1])
        qt = sb("qt", [P, KT, P])
        bd = sb("bd", [P, KT, 8, P])
        sm = sb("sm", [P, 2, 4, P])
        mx = sb("mx", [P, H1])
        nb = sb("nb", [P, H1])
        rs = sb("rs", [P, H1])
        ri = sb("ri", [P, H1])
        pr = sb("pr", [P, 2, 4, P])
        pt = sb("pt", [P, 2, 4, P])
        cx = sb("cx", [P, D])
        cxt = sb("cxt", [P, KT, P])
        xb = sb("xb", [P, D])
        x1 = sb("x1", [P, D])

        cond_in, qkv_in, rest_in, ids_in = sem("cond_in"), sem("qkv_in"), sem("rest_in"), sem("ids_in")
        xt_in, xin_in = sem("xt_in"), sem("xin_in")
        gathered = sem("gathered")
        low_ps, low_sb, yt_ps, yt_sb = sem("low_ps"), sem("low_sb"), sem("yt_ps"), sem("yt_sb")
        q_ps, kv_ps, qkv_sb = sem("q_ps"), sem("kv_ps"), sem("qkv_sb")
        rope_ab, rope_done, v_sb = sem("rope_ab"), sem("rope_done"), sem("v_sb")
        qt_ps, kt_ps, qt_sb, bd_sb = sem("qt_ps"), sem("kt_ps"), sem("qt_sb"), sem("bd_sb")
        sc_ps, masked, bias_sb, exp_done = sem("sc_ps"), sem("masked"), sem("bias_sb"), sem("exp_done")
        pt_ps, pv_done = sem("pt_ps"), sem("pv_done")
        pt_sb = [sem("pt_sb_dve"), sem("pt_sb_act")]
        ri_sb, cx_sb, cxt_ps, cxt_sb = sem("ri_sb"), sem("cx_sb"), sem("cxt_ps"), sem("cxt_sb")
        de_ps, xb_sb, x1_sb, x1_out = sem("de_ps"), sem("xb_sb"), sem("x1_sb"), sem("x1_out")
        xt_ps, xh_sb, xl_sb = sem("xt_ps"), sem("xh_sb"), sem("xl_sb")

        def slots(eng, slot):
            slot(0)
            with eng.Fori(1, B - 1) as b:
                slot(b)
            slot(B - 1)

        def has_next(b):
            return not (isinstance(b, int) and b == B - 1)

        def has_last(b):
            return not (isinstance(b, int) and b == 0)

        block = ctx.enter_context(nc.Block())
        cond_weights = ((wc, "wc"), (b_cond, "b_cond"))
        qkv_weights = ((wq, "wq"), (b_qkv, "b_qkv"), (cos, "cos"), (sin, "sin"), (ident, "ident"))
        rest = ((blocks, "blocks"), (causal, "causal"), (wd, "wd"), (b_dense, "b_dense"))
        load_tables, table_angles, table_products, table_sines = tables(nc, ctx, t, consts)

        @block.sync
        def _(sp):
            sp.dma_start(adapters[:], t["adapters"]).then_inc(ids_in, 16)
            sp.dma_start(pages[:], t["pages"]).then_inc(ids_in, 16)

            def load(b):
                wait(sp, yt_ps, b)
                wait(sp, low_sb, b)
                sp.dma_start(xt[:], t["xt"][:, :, bass.ds(b, 1), :].rearrange("p k b s -> p k (b s)")).then_inc(xt_in, 16)
                a = sp.value_load(adapters[0:1, bass.ds(b, 1)], min_val=0, max_val=7)
                sp.dma_start(la[:], t["la"][bass.ds(a, 1)].rearrange("a (k p) r -> p (a k) r", p=P)).then_inc(xt_in, 16)
                sp.dma_start(lb[:], t["lb"][bass.ds(a, 1)].rearrange("a r o -> (a r) o")).then_inc(xt_in, 16)
                sp.dma_start(ls[:], t["ls"][bass.ds(a, 1)].rearrange("a r o -> (a r) o")).then_inc(xt_in, 16)

            def load_in(b):
                wait(sp, xb_sb, b)
                sp.dma_start(xin[:], t["x"][bass.ds(b, 1)].rearrange("b s d -> (b s) d")).then_inc(xin_in, 16)

            def store(b):
                sp.wait_ge(x1_sb, b + 1)
                sp.dma_start(x1_dram[bass.ds(b, 1)].rearrange("b s d -> (b s) d"), x1[:]).then_inc(x1_out, 16)

            def gather(b):
                for j in range(NPP):
                    page = sp.value_load(pages[0:1, bass.ds(b * NPP + j, 1)], min_val=0, max_val=PAGES - 1)
                    sp.dma_start(kv_dram[bass.ds(b, 1), :, j * PSIZE:(j + 1) * PSIZE].rearrange("b g s d -> (b g) (s d)"),
                                 t["kv"][bass.ds(page, 1)].rearrange("a g s d -> (a g) (s d)")).then_inc(gathered, 16)

            sp.wait_ge(ids_in, 32)
            load(0)
            for part, signal in ((cond_weights, cond_in), (qkv_weights, qkv_in), (rest, rest_in)):
                for dst, name in part:
                    sp.dma_start(dst[:], t[name]).then_inc(signal, 16)
            for c in range(KT):
                sp.dma_start(raw[:, c], t["w2"][0, c]).then_inc(raw_in[c], 16)

            def slot(b):
                if has_next(b):
                    load(b + 1)
                load_in(b)
                gather(b)
                if has_last(b):
                    store(b - 1)

            slots(sp, slot)
            store(B - 1)
            sp.wait_ge(gathered, 16 * B * NPP)
            sp.wait_ge(x1_out, 16 * B)

        @block.tensor
        def _(pe):
            def low_rank(a):
                pe.wait_ge(xt_in, 64 * (a + 1))
                wait(pe, xl_sb, a - 2)
                for k in range(KT):
                    mm = pe.matmul(ps[0:R1, M0, 0:P], la[:, k], xt[:, k], start=k == 0, stop=k == KT - 1)
                mm.then_inc(low_ps, 1)

            def cond(a):
                pe.wait_ge(low_sb, a + 1)
                wait(pe, qt_sb, a)
                for o in range(KT):
                    for k in range(KT):
                        pe.matmul(ps[:, M1, o * P:(o + 1) * P], wc[:, k, o * P:(o + 1) * P], xt[:, k],
                                  start=k == 0, stop=False)
                    mm = pe.matmul(ps[:, M1, o * P:(o + 1) * P], lb[:, o * P:(o + 1) * P], low[:], start=False, stop=True)
                mm.then_inc(yt_ps, 1)

            def project(a):
                pe.wait_ge(yt_sb, a + 1)
                wait(pe, cxt_sb, a - 1)
                for k in range(KT):
                    mm = pe.matmul(ps[:, M2, :], yt[:, k], wq[:, k, 0:D], start=k == 0, stop=k == KT - 1)
                mm.then_inc(q_ps, 1)
                for k in range(KT):
                    mm = pe.matmul(ps[:, M1, 0:QKV1 - D], yt[:, k], wq[:, k, D:], start=k == 0, stop=k == KT - 1)
                mm.then_inc(kv_ps, 1)

            def turn(a):
                pe.wait_ge(rope_done, a + 1)
                for k in range(KT):
                    mm = pe.transpose(ps[:, M1, k * P:(k + 1) * P], qr[:, k * P:(k + 1) * P], ident[:])
                mm.then_inc(qt_ps, 1)
                flat = kr[:].rearrange("p g j d -> p (g j d)")
                for k in range(KT):
                    mm = pe.transpose(ps[:, M2, k * P:(k + 1) * P], flat[:, k * P:(k + 1) * P], ident[:])
                mm.then_inc(kt_ps, 1)

            def scores(b, c):
                if c == 0:
                    pe.wait_ge(qt_sb, b + 1)
                if c % 2 == 0:
                    pe.wait_ge(bd_sb, KT * b + c // 2 + 1)
                wait(pe, masked, 8 * b + c - 1)
                pe.matmul(ps[:, SC[c % 2], :], qt[:, c // 2], bd[:, c // 2, 4 * (c % 2):4 * (c % 2) + 4].rearrange("p j s -> p (j s)"),
                          start=True, stop=True).then_inc(sc_ps, 1)

            def turn_probs(b, c):
                pe.wait_ge(exp_done, 8 * b + c + 1)
                n = 4 * b + c // 2
                wait(pe, pt_sb[c % 2], n)
                for j in range(4):
                    mm = pe.transpose(ps[:, PT[c % 2], j * P:(j + 1) * P], pr[:, c % 2, j], ident[:])
                mm.then_inc(pt_ps, 1)

            def context(b, c):
                if c == 0:
                    wait(pe, cx_sb, b)
                    pe.wait_ge(v_sb, b + 1)
                pe.wait_ge(pt_sb[c % 2], 4 * b + c // 2 + 1)
                for j in range(4):
                    h = 4 * c + j
                    mm = pe.matmul(ps[:, CTX, h * D1:(h + 1) * D1], pt[:, c % 2, j], v[:, c], start=True, stop=True)
                mm.then_inc(pv_done, 1)

            def turn_context(d):
                pe.wait_ge(cx_sb, d + 1)
                wait(pe, bd_sb, KT * (d + 2 if has_next(d) else d + 1))
                for k in range(KT):
                    mm = pe.transpose(ps[:, M2, k * P:(k + 1) * P], cx[:, k * P:(k + 1) * P], ident[:])
                mm.then_inc(cxt_ps, 1)

            def dense(d):
                pe.wait_ge(cxt_sb, d + 1)
                if has_next(d + 1) and has_next(d):
                    pe.wait_ge(low_sb, d + 3)
                wait(pe, xl_sb, d)
                for k in range(KT):
                    mm = pe.matmul(ps[:, M0, :], cxt[:, k], wd[:, k], start=k == 0, stop=k == KT - 1)
                mm.then_inc(de_ps, 1)

            def turn_x1(d):
                pe.wait_ge(x1_sb, d + 1)
                for k in range(KT):
                    mm = pe.transpose(ps[:, M0, k * P:(k + 1) * P], x1[:, k * P:(k + 1) * P], ident[:])
                mm.then_inc(xt_ps, 1)

            def slot(b):
                nxt, last = has_next(b), has_last(b)
                scores(b, 0)
                if last:
                    context(b - 1, 7)
                if nxt:
                    low_rank(b + 1)
                scores(b, 1)
                if nxt:
                    cond(b + 1)
                if last:
                    turn_context(b - 1)
                turn_probs(b, 0)
                scores(b, 2)
                turn_probs(b, 1)
                scores(b, 3)
                if last:
                    dense(b - 1)
                context(b, 0)
                turn_probs(b, 2)
                context(b, 1)
                scores(b, 4)
                if nxt:
                    project(b + 1)
                turn_probs(b, 3)
                context(b, 2)
                scores(b, 5)
                turn_probs(b, 4)
                context(b, 3)
                if last:
                    turn_x1(b - 1)
                scores(b, 6)
                turn_probs(b, 5)
                context(b, 4)
                scores(b, 7)
                if nxt:
                    turn(b + 1)
                turn_probs(b, 6)
                context(b, 5)
                context(b, 6)
                turn_probs(b, 7)

            low_rank(0)
            pe.wait_ge(cond_in, 16 * len(cond_weights))
            cond(0)
            pe.wait_ge(qkv_in, 16 * len(qkv_weights))
            project(0)
            turn(0)
            pe.wait_ge(rest_in, 16 * len(rest))
            slots(pe, slot)
            context(B - 1, 7)
            turn_context(B - 1)
            dense(B - 1)
            turn_x1(B - 1)

        @block.scalar
        def _(act):
            def low_out(a):
                act.wait_ge(low_ps, a + 1)
                wait(act, yt_ps, a)
                act.activation(low[:], ps[0:R1, M0, 0:P], ACT.Copy, scale=ls[:, 0:1]).then_inc(low_sb, 1)

            def y_out(a):
                act.wait_ge(yt_ps, a + 1)
                wait(act, kv_ps, a)
                for o in range(KT):
                    op = act.activation(yt[:, o], ps[:, M1, o * P:(o + 1) * P], ACT.Identity, bias=b_cond[:, o:o + 1])
                op.then_inc(yt_sb, 1)

            def qt_out(a):
                act.wait_ge(qt_ps, a + 1)
                wait(act, sc_ps, 8 * a)
                act.activation(qt[:].rearrange("p k s -> p (k s)"), ps[:, M1, :], ACT.Copy).then_inc(qt_sb, 1)

            def exponent(b, c):
                act.wait_ge(bias_sb, 8 * b + c + 1)
                wait(act, pt_ps, 8 * b + c - 1)
                for j in range(4):
                    h = 4 * c + j
                    op = act.activation(pr[:, c % 2, j], sm[:, c % 2, j], ACT.Exp, bias=nb[:, h:h + 1],
                                        scale=1.0 / D1, accum_out=rs[:, h:h + 1])
                op.then_inc(exp_done, 1)

            def probs_out(b, c):
                act.wait_ge(pt_ps, 8 * b + c + 1)
                wait(act, pv_done, 8 * b + c - 1)
                act.activation(pt[:, c % 2].rearrange("p j s -> p (j s)"), ps[:, PT[c % 2], :], ACT.Copy).then_inc(pt_sb[1], 1)

            def context_out(d):
                act.wait_ge(cxt_ps, d + 1)
                wait(act, de_ps, d)
                act.activation(cxt[:].rearrange("p k s -> p (k s)"), ps[:, M2, :], ACT.Copy).then_inc(cxt_sb, 1)

            def x1_high(d):
                act.wait_ge(xt_ps, d + 1)
                act.activation(x1t_h[:, bass.ds(d, 1)].rearrange("p b k s -> p (b k s)"), ps[:, M0, :], ACT.Copy).then_inc(xh_sb, 1)

            def slot(b):
                nxt, last = has_next(b), has_last(b)
                if nxt:
                    low_out(b + 1)
                exponent(b, 0)
                exponent(b, 1)
                if nxt:
                    y_out(b + 1)
                if last:
                    context_out(b - 1)
                exponent(b, 2)
                probs_out(b, 1)
                exponent(b, 3)
                exponent(b, 4)
                probs_out(b, 3)
                exponent(b, 5)
                if last:
                    x1_high(b - 1)
                exponent(b, 6)
                probs_out(b, 5)
                if nxt:
                    qt_out(b + 1)
                exponent(b, 7)
                probs_out(b, 7)

            load_tables(act)
            low_out(0)
            act.wait_ge(cond_in, 16 * len(cond_weights))
            y_out(0)
            table_sines(act)
            qt_out(0)
            slots(act, slot)
            context_out(B - 1)
            x1_high(B - 1)

        @block.vector
        def _(dve):
            def qkv_out(a):
                dve.wait_ge(q_ps, a + 1)
                wait(dve, rope_ab, a)
                wait(dve, v_sb, a)
                dve.tensor_tensor(qkv[:, 0:D], ps[:, M2, :], b_qkv[:, 0:D], ALU.add)
                dve.wait_ge(kv_ps, a + 1)
                dve.tensor_tensor(qkv[:, D:], ps[:, M1, 0:QKV1 - D], b_qkv[:, D:], ALU.add).then_inc(qkv_sb, 1)

            def rope_sum(a):
                dve.wait_ge(rope_ab, a + 1)
                wait(dve, kt_ps, a)
                dve.tensor_tensor(qr[:], rope_a[:, 0:H1].rearrange("p h d -> p (h d)"),
                                  rope_b[:, 0:H1].rearrange("p h d -> p (h d)"), ALU.add)
                shape = [P, G1, 4, D1]
                dve.tensor_tensor(kr[:], rope_a[:, H1:].unsqueeze(2).broadcast_to(shape),
                                  rope_b[:, H1:].unsqueeze(2).broadcast_to(shape), ALU.add).then_inc(rope_done, 1)

            def keys_out(a, parts):
                dve.wait_ge(kt_ps, a + 1)
                wait(dve, sc_ps, 8 * a)
                for k in parts:
                    dve.tensor_tensor(bd[:, k], over(ps[:, M2, k * P:(k + 1) * P], 8), wide(blocks[:], P), ALU.mult).then_inc(bd_sb, 1)

            def mask(b, c):
                dve.wait_ge(sc_ps, 8 * b + c + 1)
                wait(dve, exp_done, 8 * b + c - 1)
                hold(dve)
                for j in range(4):
                    h = 4 * c + j
                    op = dve.tensor_tensor_reduce(sm[:, c % 2, j], ps[:, SC[c % 2], j * P:(j + 1) * P], causal[:], 1.0, MASKED,
                                                  ALU.add, ALU.max, mx[:, h:h + 1])
                op.then_inc(masked, 1)
                dve.wait_ge(masked, 8 * b + c + 1)
                dve.tensor_scalar(nb[:, 4 * c:4 * c + 4], mx[:, 4 * c:4 * c + 4], -1.0 / D1, None, ALU.mult).then_inc(bias_sb, 1)

            def probs_out(b, c):
                dve.wait_ge(pt_ps, 8 * b + c + 1)
                wait(dve, pv_done, 8 * b + c - 1)
                dve.tensor_copy(pt[:, c % 2].rearrange("p j s -> p (j s)"), ps[:, PT[c % 2], :]).then_inc(pt_sb[0], 1)

            def invert(b):
                dve.wait_ge(exp_done, 8 * (b + 1))
                wait(dve, cx_sb, b)
                dve.reciprocal(ri[:], rs[:]).then_inc(ri_sb, 1)

            def normalize(b):
                dve.wait_ge(ri_sb, b + 1)
                dve.wait_ge(pv_done, 8 * (b + 1))
                wait(dve, cxt_ps, b)
                dve.tensor_tensor(cx[:].rearrange("p (h d) -> p h d", d=D1), ps[:, CTX, :].rearrange("p (h d) -> p h d", d=D1),
                                  wide(ri[:], D1), ALU.mult).then_inc(cx_sb, 1)

            def residual(d):
                dve.wait_ge(de_ps, d + 1)
                dve.wait_ge(xb_sb, d + 1)
                wait(dve, xt_ps, d)
                wait(dve, x1_out, 16 * d)
                dve.tensor_tensor(x1[:], ps[:, M0, :], xb[:], ALU.add).then_inc(x1_sb, 1)

            def x1_rest(d):
                dve.wait_ge(xh_sb, d + 1)
                dve.tensor_tensor(x1t_l[:, bass.ds(d, 1)].rearrange("p b k s -> p (b k s)"), ps[:, M0, :],
                                  x1t_h[:, bass.ds(d, 1)].rearrange("p b k s -> p (b k s)"), ALU.subtract).then_inc(xl_sb, 1)

            def slot(b):
                nxt, last = has_next(b), has_last(b)
                mask(b, 0)
                if last:
                    normalize(b - 1)
                mask(b, 1)
                probs_out(b, 0)
                mask(b, 2)
                mask(b, 3)
                if last:
                    residual(b - 1)
                probs_out(b, 2)
                mask(b, 4)
                if not last:
                    table_products(dve)
                if nxt:
                    qkv_out(b + 1)
                mask(b, 5)
                probs_out(b, 4)
                mask(b, 6)
                if nxt:
                    rope_sum(b + 1)
                mask(b, 7)
                if nxt:
                    keys_out(b + 1, range(1))
                probs_out(b, 6)
                if nxt:
                    keys_out(b + 1, range(1, KT))
                if last:
                    x1_rest(b - 1)
                invert(b)

            table_angles(dve)
            dve.wait_ge(qkv_in, 16 * len(qkv_weights))
            qkv_out(0)
            rope_sum(0)
            dve.wait_ge(rest_in, 16 * len(rest))
            keys_out(0, range(KT))
            slots(dve, slot)
            normalize(B - 1)
            residual(B - 1)
            x1_rest(B - 1)

        @block.gpsimd
        def _(pool):
            def rope(a):
                pool.wait_ge(qkv_sb, a + 1)
                wait(pool, rope_done, a)
                qk = qkv[:, 0:NQK * D1].rearrange("p (h d) -> p h d", d=D1)
                half = D1 // 2
                pool.tensor_tensor(rope_a[:], qk, over(cos[:], NQK), ALU.mult)
                pool.tensor_tensor(rope_b[:, :, 0:half], qk[:, :, half:], over(sin[:, 0:half], NQK), ALU.mult)
                pool.tensor_tensor(rope_b[:, :, half:], qk[:, :, 0:half], over(sin[:, half:], NQK), ALU.mult).then_inc(rope_ab, 1)

            def values(a):
                pool.wait_ge(qkv_sb, a + 1)
                wait(pool, pv_done, 8 * a)
                hold(pool)
                pool.tensor_copy(v[:].rearrange("p g d -> p (g d)"), qkv[:, NQK * D1:]).then_inc(v_sb, 1)

            def with_bias(b):
                pool.wait_ge(xin_in, 16 * (b + 1))
                wait(pool, x1_sb, b)
                pool.tensor_tensor(xb[:], xin[:], b_dense[:], ALU.add).then_inc(xb_sb, 1)

            def slot(b):
                with_bias(b)
                if has_next(b):
                    rope(b + 1)
                    values(b + 1)

            pool.wait_ge(qkv_in, 16 * len(qkv_weights))
            rope(0)
            values(0)
            pool.wait_ge(rest_in, 16 * len(rest))
            slots(pool, slot)



def tables(nc, ctx, t, consts):
    mask_row, mask_col, cw, sw = consts
    sb = lambda n, s, d=F32: ctx.enter_context(nc.sbuf_tensor("t_" + n, s, d))
    sem = lambda n: ctx.enter_context(nc.semaphore("t_" + n))
    lens = sb("lens", [P, B], I32)
    lenf = sb("lenf", [P, B])
    key_row = sb("key_row", [P, L])
    key_col = sb("key_col", [P, LT])
    token = sb("token", [P, 1])
    inv = sb("inv", [P, HD // 2])
    norms = sb("norms", [P, 2, HD])
    pos = sb("pos", [P, B])
    angle = sb("angle", [P, B, HD // 2])
    turns = sb("turns", [P, B, HD // 2])
    sine = sb("sine", [P, B, HD // 2])
    half_sine = sb("half_sine", [P, B, HD // 2])
    minus_sine = sb("minus_sine", [P, B, HD // 2])
    cosine = sb("cosine", [P, B, HD // 2])
    loaded, step, sines = sem("loaded"), sem("step"), sem("sines")
    loads = ((lens, "lens"), (token, "token"), (inv, "inv"), (key_col, "key_col"), (norms, "norms"), (key_row, "key_row"))

    def load_tables(act):
        for dst, name in loads:
            act.dma_start(dst[:], t[name]).then_inc(loaded, 16)

    done = [0]

    def then(dve, op):
        done[0] += 1
        op.then_inc(step, 1)
        dve.wait_ge(step, done[0])

    def table_angles(dve):
        dve.wait_ge(loaded, 16 * len(loads))
        then(dve, dve.tensor_copy(lenf[:], lens[:]))
        then(dve, dve.tensor_scalar(pos[:], lenf[:], token[:, 0:1], None, ALU.add))
        then(dve, dve.tensor_tensor(angle[:], wide(pos[:], HD // 2), over(inv[:], B), ALU.mult))
        then(dve, dve.tensor_scalar(turns[:], angle[:], 1.0 / (2 * np.pi), 12582912.0, ALU.mult, ALU.add))
        then(dve, dve.tensor_scalar(turns[:], turns[:], 12582912.0, None, ALU.subtract))
        for part in TWO_PI:
            then(dve, dve.scalar_tensor_tensor(out=angle[:], in0=turns[:], scalar=-part, in1=angle[:], op0=ALU.mult, op1=ALU.add))
        then(dve, dve.tensor_scalar(angle[:], angle[:], 3.1415925, -3.1415925, ALU.min, ALU.max))
        for b in range(B):
            dve.tensor_scalar(mask_row[:, b], key_row[:], lenf[:, b:b + 1], MASKED, ALU.is_ge, ALU.mult)
            dve.tensor_scalar(mask_col[:, b], key_col[:], lenf[:, b:b + 1], MASKED, ALU.is_ge, ALU.mult)

    def table_products(dve):
        dve.wait_ge(sines, 2)
        then(dve, dve.tensor_tensor(cosine[:], half_sine[:], half_sine[:], ALU.mult))
        then(dve, dve.tensor_scalar(cosine[:], cosine[:], -2.0, 1.0, ALU.mult, ALU.add))
        then(dve, dve.tensor_scalar(minus_sine[:], sine[:], -1.0, None, ALU.mult))
        then(dve, dve.tensor_scalar(norms[:, 0], norms[:, 0], SCALE2, None, ALU.mult))
        h = HD // 2
        for kind in range(2):
            lo, hi = norms[:, kind, 0:h], norms[:, kind, h:]
            dve.tensor_tensor(cw[:, :, kind, 0:h], cosine[:], over(lo, B), ALU.mult)
            dve.tensor_tensor(cw[:, :, kind, h:], cosine[:], over(hi, B), ALU.mult)
            dve.tensor_tensor(sw[:, :, kind, 0:h], minus_sine[:], over(hi, B), ALU.mult)
            dve.tensor_tensor(sw[:, :, kind, h:], sine[:], over(lo, B), ALU.mult)

    def table_sines(act):
        act.wait_ge(step, 9)
        act.activation(sine[:], angle[:], ACT.Sin).then_inc(sines, 1)
        act.activation(half_sine[:], angle[:], ACT.Sin, scale=0.5).then_inc(sines, 1)

    return load_tables, table_angles, table_products, table_sines


def phase2_consts(nc, ctx):
    sb = lambda n, s, d: ctx.enter_context(nc.sbuf_tensor(n, s, d))
    return (sb("mask_row", [P, B, L], BF16), sb("mask_col", [P, B, LT], F32),
            sb("cw", [P, B, 2, HD], F32), sb("sw", [P, B, 2, HD], F32))


class Item:

    def __init__(self, g, b):
        self.g, self.b = (g, b) if b < B else (g + 1, b - B)
        self.n = self.g * B + self.b

    def ahead(self, k):
        return Item(self.g, self.b + k)

    def before(self):
        if isinstance(self.n, int) and self.n == 0:
            return None
        return Item(self.g, self.b - 1) if self.b else Item(self.g - 1, B - 1)

    def exists(self):
        return not (isinstance(self.g, int) and self.g >= G)


def phase2(nc, t, x1t_h, x1t_l, ident, consts, raw, raw_in, w_h, w_l, hacc, kv_dram):
    mask_row, mask_col, cw, sw = consts
    with ExitStack() as ctx:
        sb = lambda n, s, d=F32: ctx.enter_context(nc.sbuf_tensor("b_" + n, s, d))
        sem = lambda n: ctx.enter_context(nc.semaphore("b_" + n))
        ps = ctx.enter_context(nc.psum_tensor("b_ps", [P, 8, 512], F32))
        MX, ST, OT, SM, PJQ, PJK = (0, 1), (2, 3), 4, 5, 6, 7

        ones = sb("ones", [P, 1])
        minus_ones = sb("minus_ones", [P, P], F32R)
        half = sb("half", [P, REP + 1])
        wo_h, wo_l = sb("wo_h", [P, REP, D], F32R), sb("wo_l", [P, REP, D], F32R)
        cache = sb("cache", [P, LT, 2 * HD])
        ss = sb("ss", [P, REP + 1])
        rstd = sb("rstd", [P, REP + 1])
        tq = sb("tq", [P, REP + 1, HD])
        ra = sb("ra", [P, REP + 1, HD])
        rb = sb("rb", [P, REP + 1, HD])
        qt_h, qt_l = sb("qt_h", [P, 2, REP * P], F32R), sb("qt_l", [P, 2, REP * P], F32R)
        kt_h, kt_l = sb("kt_h", [P, 2, NT * P], F32R), sb("kt_l", [P, 2, NT * P], F32R)
        v_h, v_l = sb("v_h", [P, 2, LT, HD], F32R), sb("v_l", [P, 2, LT, HD], F32R)
        vn_h, vn_l = sb("vn_h", [P, 4, HD], F32R), sb("vn_l", [P, 4, HD], F32R)
        unread = sb("unread", [P, 2, L], BF16)
        m_old, m_new, m_all = sb("m_old", [P, REP]), sb("m_new", [P, REP]), sb("m_all", [P, REP])
        diag = sb("diag", [P, REP, P], F32R)
        NP, NH = 4, 4
        pf = sb("pf", [P, NP, REP * P])
        p_h, p_l = sb("p_h", [P, NH, REP * P], F32R), sb("p_l", [P, NH, REP * P], F32R)
        psum = sb("psum", [P, REP * P])
        rinv = sb("rinv", [P, REP])
        rinv_h, rinv_l = sb("rinv_h", [P, REP], F32R), sb("rinv_l", [P, REP], F32R)
        rdiag_h, rdiag_l = sb("rdiag_h", [P, REP, P], F32R), sb("rdiag_l", [P, REP, P], F32R)
        ones_r = sb("ones_r", [P, P], F32R)
        on = sb("on", [P, REP * P])
        o_h, o_l = sb("o_h", [P, REP * P], F32R), sb("o_l", [P, REP * P], F32R)

        const_sb = sem("const_sb")
        wh_sb, wl_sb, cache_in = sem("wh_sb"), sem("wl_sb"), sem("cache_in")
        k_ps, q_ps, kc_ps, qt_ps, kn_ps = sem("k_ps"), sem("q_ps"), sem("kc_ps"), sem("qt_ps"), sem("kn_ps")
        mx_ps, st_ps, pv_ps, sum_ps, wo_ps = sem("mx_ps"), sem("st_ps"), sem("pv_ps"), sem("sum_ps"), sem("wo_ps")
        vnh_sb, vnl_sb, sq_sb, tq_sb = sem("vnh_sb"), sem("vnl_sb"), sem("sq_sb"), sem("tq_sb")
        qth_sb, qtl_sb, kch_sb, kcl_sb = sem("qth_sb"), sem("qtl_sb"), sem("kch_sb"), sem("kcl_sb")
        knh_sb, knl_sb, vch_sb, vcl_sb = sem("knh_sb"), sem("knl_sb"), sem("vch_sb"), sem("vcl_sb")
        exp_sb, ph_sb, pl_sb, psum_sb = sem("exp_sb"), sem("ph_sb"), sem("pl_sb"), sem("psum_sb")
        ms_sb, rstd_sb, rab_sb, rope_sb = sem("ms_sb"), sem("rstd_sb"), sem("rab_sb"), sem("rope_sb")
        rb_sb = sem("rb_sb")
        mx_sb, mall_sb, diag_sb = sem("mx_sb"), sem("mall_sb"), sem("diag_sb")
        oraw_sb, rinv_sb, rdiag_sb, spread_ps = sem("oraw_sb"), sem("rinv_sb"), sem("rdiag_sb"), sem("spread_ps")
        rinvh_sb, rinvl_sb, rdiagl_sb = sem("rinvh_sb"), sem("rinvl_sb"), sem("rdiagl_sb")
        on_sb, oh_sb, ol_sb, h_sb = sem("on_sb"), sem("oh_sb"), sem("ol_sb"), sem("h_sb")

        def slots(eng, slot):
            def head(g):
                for b in range(B):
                    slot(Item(g, b))
            head(0)
            with eng.Fori(1, G - 1) as g:
                head(g)
            head(G - 1)

        def flat(ap):
            return ap.rearrange("p a b -> p (a b)")

        def width_of(g, c):
            if isinstance(g, int) and g == G:
                return W3
            return QKV2 if c < KT else D

        block = ctx.enter_context(nc.Block())

        @block.sync
        def _(sp):
            def chunk(g, c):
                i = 8 * g + c
                wait(sp, wl_sb, i - KT + 1)
                if isinstance(g, int) and g == G:
                    src = t["w3"][c:c + 1]
                else:
                    src = t["w2"][bass.ds(g, 1), c] if c < KT else t["wo2"][bass.ds(g, 1), c - KT]
                sp.dma_start(raw[:, c % KT, 0:src.shape[-1]], src.rearrange("g p n -> (g p) n")).then_inc(raw_in[c % KT], 16)

            def rows(m):
                wait(sp, kc_ps, m.n)
                wait(sp, vcl_sb, m.n)
                src = kv_dram[m.b, bass.ds(m.g, 1)].rearrange("g (t p) d -> p (g t) d", p=P)
                sp.dma_start(cache[:], src).then_inc(cache_in, 16)

            def slot(m):
                if m.ahead(2).exists():
                    rows(m.ahead(2))
                if m.b == 3:
                    for c in range(KT):
                        chunk(m.g + 1, c)
                if m.b == 7 and m.ahead(1).exists():
                    for c in range(KT, 2 * KT):
                        chunk(m.g + 1, c)

            rows(Item(0, 0))
            for c in range(KT, 2 * KT):
                chunk(0, c)
            rows(Item(0, 1))
            slots(sp, slot)

        @block.tensor
        def _(pe):
            def three(out, lhs, rhs, start=True, stop=True):
                pe.matmul(out, lhs[0], rhs[0], start=start, stop=False)
                pe.matmul(out, lhs[0], rhs[1], start=False, stop=False)
                return pe.matmul(out, lhs[1], rhs[0], start=False, stop=stop)

            def project(m, bank, cols, done):
                for k in range(KT):
                    if m.b == 0:
                        pe.wait_ge(wl_sb, 8 * m.g + k + 1)
                    mm = three(ps[:, bank, 0:cols.stop - cols.start], (x1t_h[:, m.b, k], x1t_l[:, m.b, k]),
                               (w_h[:, k, cols], w_l[:, k, cols]), k == 0, k == KT - 1)
                mm.then_inc(done, 1)

            def project_kv(m):
                wait(pe, knl_sb, m.n)
                project(m, PJK, slice(REP * HD, QKV2), k_ps)

            def project_q(m):
                wait(pe, qtl_sb, m.n)
                project(m, PJQ, slice(0, REP * HD), q_ps)

            def turn_cache(m):
                pe.wait_ge(cache_in, 16 * (m.n + 1))
                pe.wait_ge(tq_sb, m.n + 1)
                pe.wait_ge(vnl_sb, m.n + 1)
                for i in range(LT):
                    mm = pe.transpose(ps[:, PJK, i * P:(i + 1) * P], cache[:, i, 0:HD], ident[:])
                mm.then_inc(kc_ps, 1)

            def turn_q(m):
                pe.wait_ge(rope_sb, m.n + 1)
                for h in range(REP):
                    mm = pe.transpose(ps[:, PJQ, h * P:(h + 1) * P], ra[:, h], ident[:])
                mm.then_inc(qt_ps, 1)

            def turn_new(m):
                pe.wait_ge(kcl_sb, m.n + 1)
                pe.transpose(ps[:, PJK, 0:P], ra[:, REP], ident[:]).then_inc(kn_ps, 1)

            def row_scores(m, i):
                k = m.b % 2
                bank = MX[(NT * m.b + i) % 2]
                if i == 0:
                    pe.wait_ge(qth_sb, m.n + 1)
                    pe.wait_ge(knh_sb, m.n + 1)
                wait(pe, mx_sb, NT * m.n + i - 1)
                if i < REP:
                    mm = pe.matmul(ps[:, bank, :], qt_h[:, k, i * P:(i + 1) * P], kt_h[:, k, 0:L], start=True, stop=True)
                else:
                    for h in range(REP):
                        mm = pe.matmul(ps[:, bank, h * P:(h + 1) * P], qt_h[:, k, h * P:(h + 1) * P], kt_h[:, k, L:],
                                       start=True, stop=True)
                mm.then_inc(mx_ps, 1)

            def scores(m, i):
                k = m.b % 2
                bank = ps[:, ST[(NT * m.b + i) % 2], :]
                if i == 0:
                    pe.wait_ge(diag_sb, m.n + 1)
                    pe.wait_ge(qtl_sb, m.n + 1)
                    pe.wait_ge(knl_sb, m.n + 1)
                wait(pe, exp_sb, NT * m.n + i - 1)
                pe.matmul(bank, minus_ones[:], flat(diag[:]), start=True, stop=False)
                tile = slice(i * P, (i + 1) * P)
                three(bank, (kt_h[:, k, tile], kt_l[:, k, tile]), (qt_h[:, k], qt_l[:, k]), False).then_inc(st_ps, 1)

            def values(m, i):
                k, j = m.b % 2, (NT * m.b + i) % NH
                if i == 0:
                    wait(pe, oraw_sb, m.n)
                    pe.wait_ge(vcl_sb, m.n + 1)
                pe.wait_ge(pl_sb, NT * m.n + i + 1)
                v = (v_h[:, k, i], v_l[:, k, i]) if i < LT else (vn_h[:, m.b % 4], vn_l[:, m.b % 4])
                three(ps[:, OT, :], v, (p_h[:, j], p_l[:, j]), i == 0, i == LT).then_inc(pv_ps, 1)

            def sums(m):
                pe.wait_ge(psum_sb, LT * (m.n + 1))
                wait(pe, h_sb, m.n)
                for h in range(REP):
                    mm = pe.matmul(ps[:, SM, h:h + 1], psum[:, h * P:(h + 1) * P], ones[:], start=True, stop=True)
                mm.then_inc(sum_ps, 1)

            def spread(m):
                pe.wait_ge(rdiag_sb, m.n + 1)
                pe.wait_ge(rdiagl_sb, m.n + 1)
                pe.matmul(ps[:, SM, :], ones_r[:], flat(rdiag_h[:]), start=True, stop=False)
                pe.matmul(ps[:, SM, :], ones_r[:], flat(rdiag_l[:]), start=False, stop=True).then_inc(spread_ps, 1)

            def out_product(m):
                pe.wait_ge(ol_sb, m.n + 1)
                pe.wait_ge(wl_sb, 8 * (m.g + 1))
                for h in range(REP):
                    tile = slice(h * P, (h + 1) * P)
                    mm = three(ps[:, SM, :], (o_h[:, tile], o_l[:, tile]), (wo_h[:, h], wo_l[:, h]), h == 0, h == REP - 1)
                mm.then_inc(wo_ps, 1)

            def slot(m):
                one, two, last = m.ahead(1), m.ahead(2), m.before()
                scores(m, 0)
                scores(m, 1)
                if one.exists():
                    turn_cache(one)
                scores(m, 2)
                if last:
                    spread(last)
                values(m, 0)
                if one.exists():
                    turn_q(one)
                    turn_new(one)
                scores(m, 3)
                values(m, 1)
                if one.exists():
                    row_scores(one, 0)
                    row_scores(one, 1)
                scores(m, 4)
                values(m, 2)
                if last:
                    out_product(last)
                if one.exists():
                    row_scores(one, 2)
                if one.exists():
                    row_scores(one, 3)
                if two.exists():
                    project_q(two)
                if one.exists():
                    row_scores(one, 4)
                if two.exists():
                    project_kv(two)
                values(m, 3)
                values(m, 4)
                sums(m)

            pe.wait_ge(const_sb, 5)
            zero, one = Item(0, 0), Item(0, 1)
            project_q(zero)
            project_kv(zero)
            turn_cache(zero)
            turn_q(zero)
            turn_new(zero)
            project_q(one)
            project_kv(one)
            for i in range(NT):
                row_scores(zero, i)
            slots(pe, slot)
            spread(Item(G - 1, B - 1))
            out_product(Item(G - 1, B - 1))

        @block.scalar
        def _(act):
            def weights(g, cs):
                for c in cs:
                    i = 8 * g + c
                    act.wait_ge(raw_in[c % KT], 16 * (2 * g + c // KT + 1))
                    if c == 0:
                        wait(act, q_ps, 8 * g)
                    if c == KT:
                        wait(act, wo_ps, 8 * g)
                    width = width_of(g, c)
                    dst = w_h[:, c, 0:width] if c < KT else wo_h[:, c - KT]
                    act.activation(dst, raw[:, c % KT, 0:width], ACT.Copy).then_inc(wh_sb, 1)

            def new_kv(m):
                act.wait_ge(k_ps, m.n + 1)
                act.activation(tq[:, REP], ps[:, PJK, 0:HD], ACT.Square, accum_out=ss[:, REP:REP + 1]).then_inc(sq_sb, 1)
                wait(act, pv_ps, NT * (m.n - 3))
                act.activation(vn_h[:, m.b % 4], ps[:, PJK, HD:2 * HD], ACT.Copy).then_inc(vnh_sb, 1)

            def squares(m):
                act.wait_ge(q_ps, m.n + 1)
                wait(act, rstd_sb, m.n)
                wait(act, rb_sb, m.n)
                wait(act, rab_sb, m.n)
                for h in range(REP):
                    act.activation(tq[:, h], ps[:, PJQ, h * P:(h + 1) * P], ACT.Square, accum_out=ss[:, h:h + 1])

            def normalize(m):
                act.wait_ge(rstd_sb, m.n + 1)
                act.wait_ge(vnl_sb, m.n + 1)
                act.activation(tq[:, REP], ps[:, PJK, 0:HD], ACT.Copy, scale=rstd[:, REP:REP + 1])
                for h in range(REP):
                    op = act.activation(tq[:, h], ps[:, PJQ, h * P:(h + 1) * P], ACT.Copy, scale=rstd[:, h:h + 1])
                op.then_inc(tq_sb, 1)

            def cache_keys(m):
                act.wait_ge(kc_ps, m.n + 1)
                wait(act, st_ps, NT * (m.n - 1))
                act.activation(kt_h[:, m.b % 2, 0:L], ps[:, PJK, :], ACT.Copy).then_inc(kch_sb, 1)

            def cache_values(m):
                act.wait_ge(cache_in, 16 * (m.n + 1))
                wait(act, pv_ps, NT * (m.n - 1))
                act.activation(v_h[:, m.b % 2], cache[:, :, HD:], ACT.Copy).then_inc(vch_sb, 1)

            def queries(m):
                act.wait_ge(qt_ps, m.n + 1)
                act.activation(qt_h[:, m.b % 2], ps[:, PJQ, :], ACT.Copy).then_inc(qth_sb, 1)

            def new_keys(m):
                act.wait_ge(kn_ps, m.n + 1)
                act.activation(kt_h[:, m.b % 2, L:], ps[:, PJK, 0:P], ACT.Copy).then_inc(knh_sb, 1)

            def exponent(m, i):
                s = NT * m.b + i
                act.wait_ge(st_ps, NT * m.n + i + 1)
                wait(act, pl_sb, NT * m.n + i + 1 - NP)
                before = LT * m.n + i if i == 4 else LT * (m.n - 1) + i + 1
                before = LT * m.n + 1 if i == 4 else before
                wait(act, psum_sb, before)
                bias = mask_col[:, m.b, i:i + 1] if i < LT else 0.0
                act.activation(pf[:, s % NP], ps[:, ST[s % 2], :], ACT.Exp, bias=bias).then_inc(exp_sb, 1)

            def high(m, i):
                s = NT * m.b + i
                act.wait_ge(exp_sb, NT * m.n + i + 1)
                wait(act, pv_ps, NT * m.n + i + 1 - NH)
                act.activation(p_h[:, s % NH], pf[:, s % NP], ACT.Copy).then_inc(ph_sb, 1)

            def output_raw(m):
                act.wait_ge(pv_ps, NT * (m.n + 1))
                wait(act, ol_sb, m.n)
                act.activation(on[:], ps[:, OT, :], ACT.Copy).then_inc(oraw_sb, 1)

            def output(m):
                act.wait_ge(on_sb, m.n + 1)
                wait(act, wo_ps, m.n)
                act.activation(o_h[:], on[:], ACT.Copy).then_inc(oh_sb, 1)

            def slot(m):
                one, two = m.ahead(1), m.ahead(2)
                exponent(m, 0)
                high(m, 0)
                exponent(m, 1)
                if one.exists():
                    cache_keys(one)
                high(m, 1)
                exponent(m, 2)
                high(m, 2)
                if one.exists():
                    queries(one)
                    new_keys(one)
                if m.before():
                    output(m.before())
                exponent(m, 3)
                high(m, 3)
                if one.exists():
                    cache_values(one)
                if m.b == 6:
                    weights(m.g + 1, range(KT))
                exponent(m, 4)
                high(m, 4)
                if m.b == 0:
                    weights(m.g, range(KT, 2 * KT))
                if two.exists():
                    squares(two)
                    new_kv(two)
                output_raw(m)
                if two.exists():
                    normalize(two)

            zero, one = Item(0, 0), Item(0, 1)
            weights(0, range(KT))
            squares(zero)
            new_kv(zero)
            normalize(zero)
            cache_keys(zero)
            queries(zero)
            new_keys(zero)
            cache_values(zero)
            squares(one)
            new_kv(one)
            normalize(one)
            slots(act, slot)
            output(Item(G - 1, B - 1))

        @block.vector
        def _(dve):
            def weights(g, cs):
                for c in cs:
                    dve.wait_ge(wh_sb, 8 * g + c + 1)
                    width = width_of(g, c)
                    h, l = (w_h[:, c, 0:width], w_l[:, c, 0:width]) if c < KT else (wo_h[:, c - KT], wo_l[:, c - KT])
                    dve.tensor_tensor(l, raw[:, c % KT, 0:width], h, ALU.subtract).then_inc(wl_sb, 1)

            def new_values(m):
                dve.wait_ge(vnh_sb, m.n + 1)
                dve.tensor_tensor(vn_l[:, m.b % 4], ps[:, PJK, HD:2 * HD], vn_h[:, m.b % 4], ALU.subtract).then_inc(vnl_sb, 1)

            def cache_keys(m):
                dve.wait_ge(kch_sb, m.n + 1)
                dve.tensor_tensor(kt_l[:, m.b % 2, 0:L], ps[:, PJK, :], kt_h[:, m.b % 2, 0:L], ALU.subtract).then_inc(kcl_sb, 1)

            def rope_swapped(m):
                dve.wait_ge(tq_sb, m.n + 1)
                wait(dve, rope_sb, m.n)
                h = HD // 2
                for x, kind in ((slice(0, REP), 0), (slice(REP, REP + 1), 1)):
                    n = x.stop - x.start
                    dve.tensor_tensor(rb[:, x, 0:h], tq[:, x, h:], over(sw[:, m.b, kind, 0:h], n), ALU.mult)
                    op = dve.tensor_tensor(rb[:, x, h:], tq[:, x, 0:h], over(sw[:, m.b, kind, h:], n), ALU.mult)
                op.then_inc(rb_sb, 1)

            def rope(m):
                dve.wait_ge(rab_sb, m.n + 1)
                dve.wait_ge(rb_sb, m.n + 1)
                dve.tensor_tensor(ra[:], ra[:], rb[:], ALU.add).then_inc(rope_sb, 1)

            def queries(m):
                dve.wait_ge(qth_sb, m.n + 1)
                dve.tensor_tensor(qt_l[:, m.b % 2], ps[:, PJQ, :], qt_h[:, m.b % 2], ALU.subtract).then_inc(qtl_sb, 1)

            def new_keys(m):
                dve.wait_ge(knh_sb, m.n + 1)
                dve.tensor_tensor(kt_l[:, m.b % 2, L:], ps[:, PJK, 0:P], kt_h[:, m.b % 2, L:], ALU.subtract).then_inc(knl_sb, 1)

            def maxima(m, i):
                s = NT * m.b + i
                dve.wait_ge(mx_ps, NT * m.n + i + 1)
                bank = MX[s % 2]
                if i < REP:
                    wait(dve, mx_sb, NT * m.n + i - (1 if i else 2))
                    hold(dve)
                    dve.tensor_tensor_reduce(unread[:, i % 2], ps[:, bank, :], mask_row[:, m.b], 1.0, MASKED, ALU.add, ALU.max,
                                             m_old[:, i:i + 1]).then_inc(mx_sb, 1)
                else:
                    dve.tensor_reduce(m_new[:], ps[:, bank, :].rearrange("p (h s) -> p h s", h=REP), AX.X, ALU.max).then_inc(mx_sb, 1)

            def diagonal(m):
                dve.wait_ge(mx_sb, NT * (m.n + 1))
                dve.tensor_tensor(m_all[:], m_old[:], m_new[:], ALU.max).then_inc(mall_sb, 1)
                dve.wait_ge(mall_sb, m.n + 1)
                wait(dve, st_ps, NT * m.n)
                dve.tensor_tensor(diag[:], over(ident[:], REP), wide(m_all[:], P), ALU.mult).then_inc(diag_sb, 1)

            def low(m, i):
                s = NT * m.b + i
                dve.wait_ge(ph_sb, NT * m.n + i + 1)
                dve.tensor_tensor(p_l[:, s % NH], pf[:, s % NP], p_h[:, s % NH], ALU.subtract).then_inc(pl_sb, 1)

            def invert(m):
                dve.wait_ge(sum_ps, m.n + 1)
                wait(dve, rdiag_sb, m.n)
                wait(dve, spread_ps, m.n)
                dve.reciprocal(rinv[:], ps[:, SM, 0:REP]).then_inc(rinv_sb, 1)
                dve.wait_ge(rinv_sb, m.n + 1)
                dve.tensor_copy(rinv_h[:], rinv[:]).then_inc(rinvh_sb, 1)
                dve.wait_ge(rinvh_sb, m.n + 1)
                dve.tensor_tensor(rinv_l[:], rinv[:], rinv_h[:], ALU.subtract).then_inc(rinvl_sb, 1)
                dve.wait_ge(rinvl_sb, m.n + 1)
                dve.tensor_tensor(rdiag_l[:], over(ident[:], REP), wide(rinv_l[:], P), ALU.mult).then_inc(rdiagl_sb, 1)

            def divide(m):
                dve.wait_ge(spread_ps, m.n + 1)
                dve.wait_ge(oraw_sb, m.n + 1)
                wait(dve, ol_sb, m.n)
                dve.tensor_tensor(on[:], ps[:, SM, :], on[:], ALU.mult).then_inc(on_sb, 1)

            def output(m):
                dve.wait_ge(oh_sb, m.n + 1)
                dve.tensor_tensor(o_l[:], on[:], o_h[:], ALU.subtract).then_inc(ol_sb, 1)

            def accumulate(m):
                dve.wait_ge(wo_ps, m.n + 1)
                if not isinstance(m.n, int) or m.n:
                    wait(dve, h_sb, m.n)
                else:
                    dve.wait_ge(const_sb, 4)
                dve.tensor_tensor(hacc[:, m.b], ps[:, SM, :], hacc[:, m.b], ALU.add).then_inc(h_sb, 1)

            def slot(m):
                one, two, last = m.ahead(1), m.ahead(2), m.before()
                if last:
                    invert(last)
                if one.exists():
                    rope_swapped(one)
                low(m, 0)
                if one.exists():
                    rope(one)
                    cache_keys(one)
                low(m, 1)
                if last:
                    divide(last)
                low(m, 2)
                if one.exists():
                    queries(one)
                    new_keys(one)
                if last:
                    output(last)
                if one.exists():
                    maxima(one, 0)
                low(m, 3)
                if one.exists():
                    maxima(one, 1)
                if m.b == 6:
                    weights(m.g + 1, range(KT))
                if last:
                    accumulate(last)
                if one.exists():
                    maxima(one, 2)
                low(m, 4)
                if m.b == 0:
                    weights(m.g, range(KT, 2 * KT))
                if one.exists():
                    maxima(one, 3)
                    maxima(one, 4)
                    diagonal(one)
                if two.exists():
                    new_values(two)

            dve.memset(ones[:], 1.0).then_inc(const_sb, 1)
            dve.memset(hacc[:], 0.0).then_inc(const_sb, 1)
            dve.memset(minus_ones[:].bitcast(F32), -1.0).then_inc(const_sb, 1)
            dve.memset(ones_r[:].bitcast(F32), 1.0).then_inc(const_sb, 1)
            zero, one = Item(0, 0), Item(0, 1)
            weights(0, range(KT))
            new_values(zero)
            rope_swapped(zero)
            cache_keys(zero)
            rope(zero)
            queries(zero)
            new_keys(zero)
            new_values(one)
            for i in range(NT):
                maxima(zero, i)
            diagonal(zero)
            slots(dve, slot)
            last = Item(G - 1, B - 1)
            invert(last)
            divide(last)
            output(last)
            accumulate(last)

        @block.gpsimd
        def _(pool):
            def rms(m):
                pool.wait_ge(sq_sb, m.n + 1)
                wait(pool, tq_sb, m.n)
                hold(pool)
                pool.tensor_scalar(rstd[:], ss[:], 1.0 / HD, EPS, ALU.mult, ALU.add).then_inc(ms_sb, 1)
                pool.wait_ge(ms_sb, m.n + 1)
                pool.tensor_tensor(rstd[:], rstd[:], half[:], ALU.pow).then_inc(rstd_sb, 1)

            def rope(m):
                pool.wait_ge(tq_sb, m.n + 1)
                wait(pool, kn_ps, m.n)
                pool.tensor_tensor(ra[:, 0:REP], tq[:, 0:REP], over(cw[:, m.b, 0], REP), ALU.mult)
                pool.tensor_tensor(ra[:, REP], tq[:, REP], cw[:, m.b, 1], ALU.mult).then_inc(rab_sb, 1)

            def inverses(m):
                pool.wait_ge(rinvh_sb, m.n + 1)
                wait(pool, spread_ps, m.n)
                pool.tensor_tensor(rdiag_h[:], over(ident[:], REP), wide(rinv_h[:], P), ALU.mult).then_inc(rdiag_sb, 1)

            def cache_values(m):
                pool.wait_ge(vch_sb, m.n + 1)
                pool.tensor_tensor(v_l[:, m.b % 2], cache[:, :, HD:], v_h[:, m.b % 2], ALU.subtract).then_inc(vcl_sb, 1)

            def add(m, i):
                s = NT * m.b + i
                pool.wait_ge(exp_sb, NT * m.n + i + 1)
                if i == 1:
                    wait(pool, sum_ps, m.n)
                    first = pf[:, (s - 1) % NP]
                else:
                    pool.wait_ge(psum_sb, LT * m.n + i - 1)
                    first = psum[:]
                pool.tensor_tensor(psum[:], first, pf[:, s % NP], ALU.add).then_inc(psum_sb, 1)

            def slot(m):
                one, two, last = m.ahead(1), m.ahead(2), m.before()
                if last:
                    inverses(last)
                if one.exists():
                    rope(one)
                add(m, 1)
                add(m, 2)
                add(m, 3)
                if one.exists():
                    cache_values(one)
                add(m, 4)
                if two.exists():
                    rms(two)

            pool.memset(half[:], -0.5).then_inc(const_sb, 1)
            pool.wait_ge(const_sb, 5)
            zero, one = Item(0, 0), Item(0, 1)
            rms(zero)
            rope(zero)
            cache_values(zero)
            rms(one)
            slots(pool, slot)
            inverses(Item(G - 1, B - 1))


def phase3(nc, t, ident, w_h, w_l, hacc, x1_dram, out):
    with ExitStack() as ctx:
        sb = lambda n, s, d=F32: ctx.enter_context(nc.sbuf_tensor("c_" + n, s, d))
        sem = lambda n: ctx.enter_context(nc.semaphore("c_" + n))
        ps = ctx.enter_context(nc.psum_tensor("c_ps", [P, 8, 512], F32))
        HT, F, GL, LO = (0, 1), (2, 3), (4, 5), (6, 7)
        NX = NR + MAXR

        bt = sb("bt", [MAXR, D])
        b_ffn = sb("b_ffn", [P, D])
        b_gate = sb("b_gate", [P, NR])
        first = sb("first", [P, NR])
        most = sb("most", [P, MAXR])
        x1 = sb("x1", [P, B, D])
        ht_h, ht_l = sb("ht_h", [P, 2, KT, P], F32R), sb("ht_l", [P, 2, KT, P], F32R)
        sc = sb("sc", [P, 2, NR])
        top = sb("top", [P, 2])
        weight = sb("weight", [P, 2, NR])
        expert = sb("expert", [P, 2])
        low = sb("low", [P, 2, MAXR])
        lowt = sb("lowt", [MAXR, 2, P])
        y = sb("y", [P, 2, D])

        weights_in, x1_in, stored = sem("weights_in"), sem("x1_in"), [sem("stored0"), sem("stored1")]
        ht_ps, hth_sb, htl_sb, gl_ps, f_ps = sem("ht_ps"), sem("hth_sb"), sem("htl_sb"), sem("gl_ps"), sem("f_ps")
        sc_sb, top_sb, weight_sb = sem("sc_sb"), sem("top_sb"), sem("weight_sb")
        expert_sb, low_sb = sem("expert_sb"), sem("low_sb")
        lowt_ps, lowt_sb, xb_sb, y_sb = sem("lowt_ps"), sem("lowt_sb"), sem("xb_sb"), sem("y_sb")

        def flat(ap):
            return ap.rearrange("p a b -> p (a b)")

        block = ctx.enter_context(nc.Block())
        weights = ((bt, "bt"), (b_gate, "b_gate"), (first, "first"), (most, "most"), (b_ffn, "b_ffn"))

        @block.sync
        def _(sp):
            for dst, name in weights:
                sp.dma_start(dst[:], t[name]).then_inc(weights_in, 16)
            sp.dma_start(x1[:], x1_dram.rearrange("b s d -> s b d")).then_inc(x1_in, 16)
            for b in range(B):
                sp.wait_ge(y_sb, b + 1)
                sp.dma_start(out[b], y[:, b % 2]).then_inc(stored[b % 2], 16)
            for k in range(2):
                sp.wait_ge(stored[k], 16 * (B // 2))

        @block.tensor
        def _(pe):
            def turn(b):
                wait(pe, htl_sb, b - 1)
                for i in range(KT):
                    mm = pe.transpose(ps[:, HT[b % 2], i * P:(i + 1) * P], hacc[:, b, i * P:(i + 1) * P], ident[:])
                mm.then_inc(ht_ps, 1)

            def product(bank, b, cols, closed):
                h, l = (ht_h[:, b % 2], ht_l[:, b % 2])
                for i in range(KT):
                    pe.matmul(bank, h[:, i], w_h[:, i, cols], start=i == 0, stop=False)
                    pe.matmul(bank, h[:, i], w_l[:, i, cols], start=False, stop=False)
                    mm = pe.matmul(bank, l[:, i], w_h[:, i, cols], start=False, stop=closed and i == KT - 1)
                return mm

            def gate(b):
                pe.wait_ge(htl_sb, b + 1)
                wait(pe, low_sb, b - 1)
                product(ps[:, GL[b % 2], 0:NX], b, slice(D, W3), True).then_inc(gl_ps, 1)

            def ffn(b):
                wait(pe, y_sb, b - 1)
                product(ps[:, F[b % 2], :], b, slice(0, D), False)

            def low_rank(b):
                k = b % 2
                pe.wait_ge(low_sb, b + 1)
                wait(pe, lowt_sb, b - 1)
                pe.transpose(ps[0:MAXR, LO[k], 0:P], low[:, k], ident[:]).then_inc(lowt_ps, 1)

            def add_low_rank(b):
                pe.wait_ge(lowt_sb, b + 1)
                pe.matmul(ps[:, F[b % 2], :], lowt[:, b % 2], bt[:], start=False, stop=True).then_inc(f_ps, 1)

            turn(0)
            turn(1)
            gate(0)
            for b in range(B):
                ffn(b)
                if b == 0:
                    pe.wait_ge(weights_in, 16 * len(weights))
                low_rank(b)
                if b + 1 < B:
                    gate(b + 1)
                if b + 2 < B:
                    turn(b + 2)
                add_low_rank(b)

        @block.scalar
        def _(act):
            def h_out(b):
                act.wait_ge(ht_ps, b + 1)
                wait(act, f_ps, b - 1)
                act.activation(flat(ht_h[:, b % 2]), ps[:, HT[b % 2], :], ACT.Copy).then_inc(hth_sb, 1)

            h_out(0)
            h_out(1)
            for b in range(B):
                act.wait_ge(lowt_ps, b + 1)
                act.activation(lowt[:, b % 2], ps[0:MAXR, LO[b % 2], 0:P], ACT.Copy).then_inc(lowt_sb, 1)
                if b + 2 < B:
                    h_out(b + 2)

        @block.vector
        def _(dve):
            def h_rest(b):
                dve.wait_ge(hth_sb, b + 1)
                dve.tensor_tensor(flat(ht_l[:, b % 2]), ps[:, HT[b % 2], :], flat(ht_h[:, b % 2]), ALU.subtract).then_inc(htl_sb, 1)

            h_rest(0)
            dve.wait_ge(weights_in, 16 * len(weights))
            for b in range(B):
                k = b % 2
                dve.wait_ge(gl_ps, b + 1)
                dve.tensor_tensor(sc[:, k], ps[:, GL[k], 0:NR], b_gate[:], ALU.add).then_inc(sc_sb, 1)
                dve.wait_ge(sc_sb, b + 1)
                dve.tensor_reduce(top[:, k:k + 1], sc[:, k], AX.X, ALU.max).then_inc(top_sb, 1)
                dve.wait_ge(top_sb, b + 1)
                dve.scalar_tensor_tensor(out=weight[:, k], in0=sc[:, k], scalar=top[:, k:k + 1], in1=first[:],
                                         op0=ALU.is_ge, op1=ALU.mult).then_inc(weight_sb, 1)
                dve.wait_ge(weight_sb, b + 1)
                dve.tensor_reduce(expert[:, k:k + 1], weight[:, k], AX.X, ALU.max).then_inc(expert_sb, 1)
                dve.wait_ge(expert_sb, b + 1)
                wait(dve, lowt_ps, b - 1)
                dve.scalar_tensor_tensor(out=low[:, k], in0=most[:], scalar=expert[:, k:k + 1], in1=ps[:, GL[k], NR:NX],
                                         op0=ALU.is_ge, op1=ALU.mult).then_inc(low_sb, 1)
                if b + 1 < B:
                    h_rest(b + 1)
                dve.wait_ge(f_ps, b + 1)
                dve.wait_ge(xb_sb, b + 1)
                wait(dve, stored[k], 16 * (b // 2))
                dve.tensor_tensor(y[:, k], ps[:, F[k], :], x1[:, b], ALU.add).then_inc(y_sb, 1)

        @block.gpsimd
        def _(pool):
            pool.wait_ge(weights_in, 16 * len(weights))
            pool.wait_ge(x1_in, 16)
            for b in range(B):
                pool.tensor_tensor(x1[:, b], x1[:, b], b_ffn[:], ALU.add).then_inc(xb_sb, 1)


def build_program(nc, t, out):
    x1_dram = nc.dram_tensor("x1", [B, S, D], F32).ap()
    kv_dram = nc.dram_tensor("kv_of_batch", [B, G, L, 2 * HD], F32).ap()
    with ExitStack() as ctx:
        sb = lambda n, s, d=F32: ctx.enter_context(nc.sbuf_tensor(n, s, d))
        ident = sb("ident", [P, P])
        raw = sb("raw", [P, KT, QKV2])
        raw_in = [ctx.enter_context(nc.semaphore(f"raw_in{c}")) for c in range(KT)]
        with ExitStack() as inner:
            sb2 = lambda n, s, d: inner.enter_context(nc.sbuf_tensor(n, s, d))
            x1t_h = sb2("x1t_h", [P, B, KT, P], F32R)
            x1t_l = sb2("x1t_l", [P, B, KT, P], F32R)
            consts = phase2_consts(nc, inner)
            phase1(nc, t, x1t_h, x1t_l, ident, consts, raw, raw_in, x1_dram, kv_dram)
            hacc = sb2("hacc", [P, B, D], F32)
            w_h = sb2("w_h", [P, KT, QKV2], F32R)
            w_l = sb2("w_l", [P, KT, QKV2], F32R)
            phase2(nc, t, x1t_h, x1t_l, ident, consts, raw, raw_in, w_h, w_l, hacc, kv_dram)
            phase3(nc, t, ident, w_h, w_l, hacc, x1_dram, out)


def host_arrays(**i):
    f = lambda a: np.ascontiguousarray(a)
    arange = lambda n: np.arange(n, dtype=np.float32)
    t = {}
    t["x"] = f(i["x"])
    t["xt"] = f(i["x"].reshape(B, S, KT, P).transpose(3, 2, 0, 1))
    rows = lambda w: f(w.T.reshape(KT, P, w.shape[0]).transpose(1, 0, 2))
    t["wc"] = rows(i["L0_cond_weight"])
    t["b_cond"] = f(i["L0_cond_bias"].reshape(KT, P).T)
    t["la"] = f(i["L0_cond_lora_a_weights"].transpose(0, 2, 1))
    t["lb"] = f(i["L0_cond_lora_b_weights"].transpose(0, 2, 1))
    t["ls"] = f(np.broadcast_to(i["L0_cond_scaling_factors"].reshape(8, 1, 1), (8, R1, 1)))
    t["adapters"] = f(i["itok_B_1_7"].reshape(1, B))
    t["pages"] = f(i["itok_Bx16_0_63"].reshape(1, B * NPP))

    def by_kind(w):
        w = w.reshape(G1, 6, D1, *w.shape[1:])
        return np.concatenate([w[:, 0:4].reshape(H1 * D1, *w.shape[3:]), w[:, 4].reshape(G1 * D1, *w.shape[3:]),
                               w[:, 5].reshape(G1 * D1, *w.shape[3:])])

    t["wq"] = rows(by_kind(i["L0_attn_w_qkv"]))
    t["b_qkv"] = f(np.broadcast_to(by_kind(i["L0_attn_b_qkv"]), (P, QKV1)))
    t["wd"] = rows(i["L0_attn_w_dense"])
    t["b_dense"] = f(np.broadcast_to(i["L0_attn_b_dense"], (P, D)))
    freqs = np.outer(arange(S), np.float32(1.0) / np.float32(1000000.0) ** (np.arange(0, D1, 2, dtype=np.float32) / np.float32(D1)))
    t["cos"] = f(np.concatenate([np.cos(freqs), np.cos(freqs)], 1).astype(np.float32))
    t["sin"] = f(np.concatenate([-np.sin(freqs), np.sin(freqs)], 1).astype(np.float32))
    t["causal"] = np.where(np.tri(S, dtype=bool), np.float32(0), np.float32(MASKED))
    t["blocks"] = np.kron(np.eye(8, dtype=np.float32), np.ones((D1, 1), np.float32))
    t["ident"] = np.eye(P, dtype=np.float32)
    heads = lambda w, n: w.reshape(G, n * HD, D)
    w2 = np.concatenate([heads(i["L0_cond2_Wq"], REP), heads(i["L0_cond2_Wk"], 1), heads(i["L0_cond2_Wv"], 1)], 1)
    t["w2"] = f(w2.transpose(0, 2, 1).reshape(G, KT, P, QKV2))
    t["wo2"] = f(i["L0_cond2_Wo"].T.reshape(G, REP, HD, D))
    t["lens"] = f(np.broadcast_to(i["itok_B_207_1644"], (P, B)))
    t["key_row"] = f(np.broadcast_to(arange(L), (P, L)))
    t["key_col"] = f(arange(L).reshape(LT, P).T)
    t["token"] = arange(S).reshape(P, 1)
    t["inv"] = f(np.broadcast_to(np.float32(1.0) / np.float32(10000.0) ** (np.arange(0, HD, 2, dtype=np.float32) / np.float32(HD)), (P, HD // 2)))
    t["norms"] = f(np.broadcast_to(np.stack([i["L0_cond2_q_norm_w"], i["L0_cond2_k_norm_w"]]), (P, 2, HD)))
    w3 = np.concatenate([i["L0_ffn_W"], i["L0_ffn_gate_w"], i["L0_ffn_A"]])
    t["w3"] = f(w3.T.reshape(KT, P, W3))
    t["bt"] = f(i["L0_ffn_B"].T)
    t["b_ffn"] = f(np.broadcast_to(i["L0_ffn_b"], (P, D)))
    t["b_gate"] = f(np.broadcast_to(i["L0_ffn_gate_b"], (P, NR)))
    t["first"] = f(np.broadcast_to(NR - arange(NR), (P, NR)))
    keeps = np.array([NR - min(j for j in range(NR) if RANKS[j] > r) for r in range(MAXR)], np.float32)
    t["most"] = f(np.broadcast_to(keeps, (P, MAXR)))
    t["kv"] = f(np.concatenate([i["L0_cond2_k_cache"], i["L0_cond2_v_cache"]], -1).transpose(0, 2, 1, 3))
    return t



def kernel(**inputs):
    import concourse.bacc as bacc
    from concourse.bass_utils import run_bass_kernel_spmd

    nc = bacc.Bacc("TRN2", target_bir_lowering=False, num_devices=1)
    arrays = host_arrays(**{name: np.asarray(a) for name, a in inputs.items()})
    t = {name: nc.dram_tensor(f"in_{name}", a.shape, mybir.dt.from_np(a.dtype), kind="ExternalInput").ap()
         for name, a in arrays.items()}
    out = nc.dram_tensor("out", [B, S, D], F32, kind="ExternalOutput").ap()
    build_program(nc, t, out)
    got = run_bass_kernel_spmd(nc, [{f"in_{name}": a for name, a in arrays.items()}], core_ids=[0])
    return got.results[0]["out"]
```
